# Optimizing a Trainium2 kernel written in Bass

```python
import numpy as np
import jax
import jax.numpy as jnp

def _softmax(x, axis=-1):
    return jax.nn.softmax(x, axis=axis)

def _gelu(x):
    return jax.nn.gelu(x, approximate=True)

def _silu(x):
    return jax.nn.silu(x)

def _sigmoid(x):
    return jax.nn.sigmoid(x)

def _layernorm(x, axis=-1, eps=1e-05):
    m = jnp.mean(x, axis=axis, keepdims=True)
    v = jnp.var(x, axis=axis, keepdims=True)
    return (x - m) / jnp.sqrt(v + eps)

def _scatter_add(tgt, idx, src, axis=0):
    return tgt.at[idx].add(src)

def _segment_sum(src, seg, n):
    return jax.ops.segment_sum(src, seg, n)
kernel_name = 'mk_decoder_postln_d1_seqx_r4_fe1883'

def setup_inputs(seed: int=0):
    np.random.seed(seed)
    _w = jnp.asarray

    def _rec_inputs():
        import jax
        import jax.numpy as jnp
        _rk = jax.random.key(seed)
        x = -0.0002928 + 1 * jax.random.normal(jax.random.fold_in(_rk, 1), (16, 256, 256), jnp.float32)
        _lenS = 256 - jax.random.randint(jax.random.fold_in(_rk, 7), (16,), 0, max(1, 256 // 4) + 1, jnp.int32)
        _lenS2 = 77 - jax.random.randint(jax.random.fold_in(_rk, 8), (16,), 0, max(1, 77 // 4) + 1, jnp.int32)
        _ctx_1024P = jax.random.normal(jax.random.fold_in(_rk, 11), (16, 16, 256), jnp.float32)
        _ctx_1024c = jax.random.dirichlet(jax.random.fold_in(_rk, 511), 0.3 * jnp.ones((16,), jnp.float32), (16, 77))
        _ctx_1024t = jnp.einsum('bsk,bkd->bsd', _ctx_1024c, _ctx_1024P)
        _ctx_1024t = _ctx_1024t * jax.lax.rsqrt(jnp.mean(jnp.square(_ctx_1024t)) + 1e-12) * 0.953939
        ctx_1024 = -1.39393e-06 + 0.999914 * (_ctx_1024t + 0.3 * jax.random.normal(jax.random.fold_in(_rk, 611), (16, 77, 256), jnp.float32))
        _validS = jnp.arange(256)[None, :] < _lenS[:, None]
        _validS2 = jnp.arange(77)[None, :] < _lenS2[:, None]
        _causal = jnp.tril(jnp.ones((256, 256), dtype=bool))
        mask_1x1xSxS2_ik0 = jnp.where(jnp.broadcast_to(_validS2[0:1, None, None, :], (1, 1, 256, 77)), 0, 1).astype(jnp.int32)
        return (x, ctx_1024, mask_1x1xSxS2_ik0)
    x, ctx_1024, mask_1x1xSxS2_ik0 = _rec_inputs()

    def _L0_attn_setup():
        import jax, jax.numpy as jnp
        import numpy as np
        B, T, E = (4, 512, 256)
        H, HS = (16, 64)
        key = jax.random.key(seed)
        ks = jax.random.split(key, 6)
        return {'x': jax.random.normal(ks[0], (B, T, E), dtype=jnp.float32), 'Wq': jax.random.normal(ks[1], (H, E, HS), dtype=jnp.float32) * 0.02, 'Wk': jax.random.normal(ks[2], (H, E, HS), dtype=jnp.float32) * 0.02, 'Wv': jax.random.normal(ks[3], (H, E, HS), dtype=jnp.float32) * 0.02, 'proj_w': jax.random.normal(ks[4], (E, H * HS), dtype=jnp.float32) * 0.02, 'proj_b': jax.random.normal(ks[5], (E,), dtype=jnp.float32) * 0.02}
    _L0_attn_all = _L0_attn_setup()
    _L0_attn_in = {k: v for k, v in _L0_attn_all.items() if k in ('Wq', 'Wk', 'Wv', 'proj_w', 'proj_b')}
    del _L0_attn_all

    def _L0_xattn_setup():
        import jax, jax.numpy as jnp
        import numpy as np
        NUM_HEAD = 16
        DIM_MODEL = 256
        D_K = DIM_MODEL // NUM_HEAD
        NEG = -1000000000.0
        key = jax.random.key(seed)
        ks = jax.random.split(key, 8)
        B, S, D = (2, 512, DIM_MODEL)
        q = jax.random.normal(ks[0], (B, S, D), dtype=jnp.float32)
        k = jax.random.normal(ks[1], (B, S, D), dtype=jnp.float32)
        v = jax.random.normal(ks[2], (B, S, D), dtype=jnp.float32)
        mask = jnp.tril(jnp.ones((S, S), dtype=jnp.int32))[None, None]
        scale = 1.0 / np.sqrt(D)
        w_q = jax.random.normal(ks[3], (D, D), dtype=jnp.float32) * scale
        w_k = jax.random.normal(ks[4], (D, D), dtype=jnp.float32) * scale
        w_v = jax.random.normal(ks[5], (D, D), dtype=jnp.float32) * scale
        w_o = jax.random.normal(ks[6], (D, D), dtype=jnp.float32) * scale
        return {'q': q, 'k': k, 'v': v, 'mask': mask, 'w_q': w_q, 'w_k': w_k, 'w_v': w_v, 'w_o': w_o}
    _L0_xattn_all = _L0_xattn_setup()
    _L0_xattn_in = {k: v for k, v in _L0_xattn_all.items() if k in ('w_q', 'w_k', 'w_v', 'w_o')}
    del _L0_xattn_all

    def _L0_ffn_setup():
        import jax, jax.numpy as jnp
        import numpy as np
        E = 8
        TOP_K = 2
        CAP_FACTOR = 1.25
        MIN_CAP = 4
        SCORE_SCALE = 1.0

        def _ffn(x, w1, b1, w2, b2):
            return jax.nn.gelu(x @ w1 + b1, approximate=False) @ w2 + b2
        key = jax.random.key(seed)
        ks = jax.random.split(key, 6)
        B, S, D, I = (4, 512, 256, 1024)
        std = 0.02
        return {'x': jax.random.normal(ks[0], (B, S, D), jnp.float32), 'Wr': jax.random.normal(ks[1], (E, D), jnp.float32) * std, 'W1': jax.random.normal(ks[2], (E, D, I), jnp.float32) * std, 'b1': jnp.zeros((E, I), jnp.float32), 'W2': jax.random.normal(ks[3], (E, I, D), jnp.float32) * std, 'b2': jnp.zeros((E, D), jnp.float32), 'fw1': jax.random.normal(ks[4], (D, I), jnp.float32) * std, 'fb1': jnp.zeros((I,), jnp.float32), 'fw2': jax.random.normal(ks[5], (I, D), jnp.float32) * std, 'fb2': jnp.zeros((D,), jnp.float32)}
    _L0_ffn_all = _L0_ffn_setup()
    _L0_ffn_in = {k: v for k, v in _L0_ffn_all.items() if k in ('Wr', 'W1', 'b1', 'W2', 'b2', 'fw1', 'fb1', 'fw2', 'fb2')}
    del _L0_ffn_all
    return {'x': x, 'ctx_1024': ctx_1024, 'mask_1x1xSxS2_ik0': mask_1x1xSxS2_ik0, 'L0_attn_Wq': _L0_attn_in['Wq'], 'L0_attn_Wk': _L0_attn_in['Wk'], 'L0_attn_Wv': _L0_attn_in['Wv'], 'L0_attn_proj_w': _L0_attn_in['proj_w'], 'L0_attn_proj_b': _L0_attn_in['proj_b'], 'L0_xattn_w_q': _L0_xattn_in['w_q'], 'L0_xattn_w_k': _L0_xattn_in['w_k'], 'L0_xattn_w_v': _L0_xattn_in['w_v'], 'L0_xattn_w_o': _L0_xattn_in['w_o'], 'L0_ffn_Wr': _L0_ffn_in['Wr'], 'L0_ffn_W1': _L0_ffn_in['W1'], 'L0_ffn_b1': _L0_ffn_in['b1'], 'L0_ffn_W2': _L0_ffn_in['W2'], 'L0_ffn_b2': _L0_ffn_in['b2'], 'L0_ffn_fw1': _L0_ffn_in['fw1'], 'L0_ffn_fb1': _L0_ffn_in['fb1'], 'L0_ffn_fw2': _L0_ffn_in['fw2'], 'L0_ffn_fb2': _L0_ffn_in['fb2']}

def reference(x, ctx_1024, mask_1x1xSxS2_ik0, L0_attn_Wq, L0_attn_Wk, L0_attn_Wv, L0_attn_proj_w, L0_attn_proj_b, L0_xattn_w_q, L0_xattn_w_k, L0_xattn_w_v, L0_xattn_w_o, L0_ffn_Wr, L0_ffn_W1, L0_ffn_b1, L0_ffn_W2, L0_ffn_b2, L0_ffn_fw1, L0_ffn_fb1, L0_ffn_fw2, L0_ffn_fb2):
    import jax
    import jax.numpy as jnp

    def _L0_attn_ref(x, Wq, Wk, Wv, proj_w, proj_b):
        import jax, jax.numpy as jnp
        import numpy as np
        B, T, E = (4, 512, 256)
        H, HS = (16, 64)
        b, t, e = x.shape
        h, _, hs = Wq.shape
        q = jnp.einsum('bxy,iyk->bxik', x, Wq).reshape(h, b, t, hs)
        k = jnp.einsum('bxy,iyk->bxik', x, Wk).reshape(h, b, t, hs)
        v = jnp.einsum('bxy,iyk->bxik', x, Wv).reshape(h, b, t, hs)
        wei = jnp.einsum('hbqd,hbkd->hbqk', q, k) * hs ** (-0.5)
        causal = jnp.tril(jnp.ones((t, t), dtype=bool))
        wei = jnp.where(causal, wei, -jnp.inf)
        wei = jax.nn.softmax(wei, axis=-1)
        out = jnp.einsum('hbqk,hbkd->hbqd', wei, v)
        out = out.reshape(b, t, h * hs)
        out = out @ proj_w.T + proj_b
        return out

    def _L0_xattn_ref(q, k, v, mask, w_q, w_k, w_v, w_o):
        import jax, jax.numpy as jnp
        import numpy as np
        NUM_HEAD = 16
        DIM_MODEL = 256
        D_K = DIM_MODEL // NUM_HEAD
        NEG = -1000000000.0
        B, S, D = q.shape
        H, dk = (NUM_HEAD, D_K)

        def proj(x, w):
            return (x @ w.T).reshape(B, -1, H, dk).transpose(0, 2, 1, 3)
        Q, K, V = (proj(q, w_q), proj(k, w_k), proj(v, w_v))
        scores = jnp.einsum('bhqd,bhkd->bhqk', Q, K) / jnp.sqrt(jnp.float32(dk))
        scores = jnp.where(mask == 0, NEG, scores)
        attn = jax.nn.softmax(scores, axis=-1)
        out = jnp.einsum('bhqk,bhkd->bhqd', attn, V)
        out = out.transpose(0, 2, 1, 3).reshape(B, S, D)
        return out @ w_o.T

    def _L0_ffn_ref(x, Wr, W1, b1, W2, b2, fw1, fb1, fw2, fb2):
        import jax, jax.numpy as jnp
        import numpy as np
        E = 8
        TOP_K = 2
        CAP_FACTOR = 1.25
        MIN_CAP = 4
        SCORE_SCALE = 1.0

        def _ffn(x, w1, b1, w2, b2):
            return jax.nn.gelu(x @ w1 + b1, approximate=False) @ w2 + b2
        B, S, D = x.shape
        T = B * S
        x_flat = x.reshape(T, D)
        logits = x_flat @ Wr.T * SCORE_SCALE
        probs = jax.nn.softmax(logits, axis=-1)
        topk_scores, topk_experts = jax.lax.top_k(probs, TOP_K)
        topk_scores = topk_scores / jnp.clip(topk_scores.sum(-1, keepdims=True), 1e-09, None)
        cap = max(int(CAP_FACTOR * (T * TOP_K / E)), MIN_CAP)
        y_fb = _ffn(x_flat, fw1, fb1, fw2, fb2)
        y_flat = jnp.zeros_like(x_flat)
        fallback = jnp.zeros((T,), bool)
        tok_ids = jnp.arange(T, dtype=jnp.int32)
        for e in range(E):
            match = topk_experts == e
            elig = match.any(-1) & ~fallback
            pos = jnp.cumsum(elig) - 1
            kept = elig & (pos < cap)
            overflow = elig & (pos >= cap)
            slot = jnp.where(kept, pos, cap)
            buf = jnp.zeros((cap + 1,), jnp.int32).at[slot].set(tok_ids)
            vmask = jnp.zeros((cap + 1,), bool).at[slot].set(kept)
            idx = buf[:cap]
            valid = vmask[:cap]
            x_e = x_flat[idx]
            y_e = _ffn(x_e, W1[e], b1[e], W2[e], b2[e])
            w_tok = (topk_scores * match).sum(-1)
            w = jnp.where(valid, w_tok[idx], 0.0)
            y_flat = y_flat.at[idx].add(y_e * w[:, None])
            y_flat = jnp.where(overflow[:, None], y_fb, y_flat)
            fallback = fallback | overflow
        return y_flat.reshape(B, S, D)
    x = _layernorm(x + _L0_attn_ref(x, L0_attn_Wq, L0_attn_Wk, L0_attn_Wv, L0_attn_proj_w, L0_attn_proj_b), axis=-1)
    x = _layernorm(x + _L0_xattn_ref(x, ctx_1024, ctx_1024, mask_1x1xSxS2_ik0, L0_xattn_w_q, L0_xattn_w_k, L0_xattn_w_v, L0_xattn_w_o), axis=-1)
    x = _layernorm(x + _L0_ffn_ref(x, L0_ffn_Wr, L0_ffn_W1, L0_ffn_b1, L0_ffn_W2, L0_ffn_b2, L0_ffn_fw1, L0_ffn_fb1, L0_ffn_fw2, L0_ffn_fb2), axis=-1)
    return x

_drawn_inputs = setup_inputs


def setup_inputs(seed=0):
    import zlib

    import numpy as np

    out = dict(_drawn_inputs(seed))
    spreads = {'L0_ffn_b1': (0.0, 0.307),
     'L0_ffn_b2': (0.0, 0.1),
     'L0_ffn_fb1': (0.0, 0.1),
     'L0_ffn_fb2': (0.0, 0.1)}
    factors = {'L0_attn_Wq': 8.0, 'L0_attn_Wk': 8.0, 'L0_attn_proj_b': 2.681}
    for name, (base, spread) in spreads.items():
        noise = np.random.default_rng([zlib.crc32(name.encode()), seed]).standard_normal(out[name].shape)
        drawn = base * np.exp(spread * noise) if base else spread * noise
        out[name] = jnp.asarray(drawn.astype(out[name].dtype))
    for name, factor in factors.items():
        out[name] = (out[name] * factor).astype(out[name].dtype)
    return out
```

```python
from contextlib import ExitStack

import concourse.bass as bass
from concourse import mybir

F32 = mybir.dt.float32
F16 = mybir.dt.float16
I32 = mybir.dt.int32
U32 = mybir.dt.uint32
ALU = mybir.AluOpType
ACT = mybir.ActivationFunctionType
AX = mybir.AxisListType

P = 128
BATCH, SEQ, D = 16, 256, 256
TOKENS = BATCH * SEQ
TILES = TOKENS // P
H, HS = 16, 64
GTOK = SEQ // H
GROUPS = P // GTOK
KC = D // P
CTX, DK = 77, 16
HB = P // DK
E = 8
NE = E + 1
FF = 1024
WSIZE = 2 * D * FF // P
PIECES = TILES - 8
PIECE = NE * WSIZE // PIECES
FC = FF // P
CAP = int(1.25 * (TOKENS * 2 / E))
EPS = 1e-5

X_UP = 4.0
WA_UP = 16.0
WP_UP = 64.0
QK_UP = X_UP * WA_UP
SCORE_SCALE = HS ** -0.5 / QK_UP ** 2
SCORE2_SCALE = DK ** -0.5 / QK_UP ** 2
NEG2 = -1e9 / SCORE2_SCALE

FILLS = [("v", 0), ("q", 0), ("v", 1), ("q", 1), ("q", 2), ("q", 3), ("k", 0), ("k", 1), ("k", 2), ("k", 3)]
NF = len(FILLS)
V_FILLS = 3
FILLS_OF_SLOT = [[0, 1], [2, 3], [4], [5], [6], [7], [8], [9]]


def attention_block(nc, ctx, io, keep):
    def sb(name, shape, dt):
        return ctx.enter_context(nc.sbuf_tensor(name, shape, dt))

    def sem(name):
        return ctx.enter_context(nc.semaphore(name))

    wqk = {n: sb("w2_" + n, [P, 2, KC, H, 2, HS], F16) for n in "qk"}
    wv = sb("wv_pair", [P, 2, KC, H * HS], F16)
    wp = sb("proj_pair", [P, 2, H, D], F16)
    w2 = {n: sb("xw_" + n, [P, 2, KC, D], F16) for n in ("q", "k", "v", "o")}
    wr = sb("wr", [P, KC, E], F32)
    proj_b = sb("proj_b", [P, D], F32)
    ident = keep["ident"]
    ident16 = keep["ident16"]
    ident_big = sb("ident_big", [P, P], F16)
    causal = sb("causal", [P, P], F16)
    lo_rows = sb("lo_rows", [P, 1], F32)
    head_rows = sb("head_rows", [P, HB, CTX], F16)
    mask = sb("mask", [P, 2, CTX], I32)
    neg_half = keep["neg_half"]
    s_held_dve, s_held_pool, s_held_sp = keep["s_held_dve"], keep["s_held_pool"], keep["s_held_sp"]

    with ExitStack() as tmp:
        stage = {n: tmp.enter_context(nc.sbuf_tensor("st_" + n, [P, KC, D * 4], F32)) for n in "qkv"}
        stage_p = tmp.enter_context(nc.sbuf_tensor("st_p", [P, H, D], F32))
        stage_x = {n: tmp.enter_context(nc.sbuf_tensor("st_x" + n, [P, KC, D], F32)) for n in ("q", "k", "v", "o")}
        ld = {n: tmp.enter_context(nc.semaphore("ld_" + n)) for n in ("q", "k", "v", "p", "xq", "xk", "xv", "xo")}
        s_small = tmp.enter_context(nc.semaphore("s_small"))
        s_hi = tmp.enter_context(nc.semaphore("s_hi"))
        s_lo = tmp.enter_context(nc.semaphore("s_lo"))
        s_const = tmp.enter_context(nc.semaphore("s_const"))
        s_zero = tmp.enter_context(nc.semaphore("s_zero"))
        s_z_out = tmp.enter_context(nc.semaphore("s_z_out"))
        zero = tmp.enter_context(nc.sbuf_tensor("zero", [P, 8 * D], F32))
        block = tmp.enter_context(nc.Block())

        @block.sync
        def _(sp):
            for n in "qkv":
                sp.dma_start(stage[n][:], io["w" + n].rearrange("(c p) n -> p c n", p=P)).then_inc(ld[n], 16)
            for half in range(2):
                sp.dma_start(stage_p[half * HS:(half + 1) * HS], io["proj"].rearrange("(h d) n -> d h n", d=HS)).then_inc(ld["p"], 16)
            for n in ("q", "k", "v", "o"):
                sp.dma_start(stage_x[n][:], io["xw" + n].rearrange("(c p) n -> p c n", p=P)).then_inc(ld["x" + n], 16)
            sp.dma_start(wr[:], io["wr"].rearrange("(c p) n -> p c n", p=P)).then_inc(s_small, 16)
            sp.dma_start(proj_b[:], io["proj_b"].rearrange("(a n) -> a n", a=1).partition_broadcast(P)[:, 0, :]).then_inc(s_small, 16)
            sp.dma_start(mask[:], io["mask"].rearrange("(c p) k -> p c k", p=P)).then_inc(s_small, 16)
            sp.wait_ge(s_small, 48)

        pairs = []
        for n in "qk":
            for copy in range(2):
                pairs.append((ld[n], 16, stage[n][:].rearrange("p c (h d) -> p c h d", d=HS),
                              [wqk[n][:, k, :, :, copy, :] for k in range(2)], WA_UP))
        pairs.append((ld["v"], 16, stage["v"][:], [wv[:, k] for k in range(2)], WA_UP))
        pairs.append((ld["p"], 32, stage_p[:], [wp[:, k] for k in range(2)], WP_UP))
        for n in ("q", "k", "v", "o"):
            pairs.append((ld["x" + n], 16, stage_x[n][:], [w2[n][:, k] for k in range(2)], WA_UP))

        @block.scalar
        def _(act):
            act.wait_ge(s_zero, 1)
            z = io["z_scr"].rearrange("(p n) d -> p (n d)", p=P)
            for n in range(0, z.shape[1], 8 * D):
                act.dma_start(z[:, n:n + 8 * D], zero[:]).then_inc(s_z_out, 16)
            for s, v, src, (hi, lo), up in pairs:
                act.wait_ge(s, v)
                for c in range(src.shape[1]):
                    last = nc.scalar.activation(hi[:, c], src[:, c], ACT.Copy, scale=up)
                last.then_inc(s_hi, 1)
            act.wait_ge(s_z_out, 16 * (z.shape[1] // (8 * D)))

        @block.vector
        def _(dve):
            for n, (s, v, src, (hi, lo), up) in enumerate(pairs):
                dve.wait_ge(s, v)
                dve.wait_ge(s_hi, n + 1)
                for c in range(src.shape[1]):
                    nc.vector.scalar_tensor_tensor(out=lo[:, c], in0=src[:, c], scalar=up, in1=hi[:, c],
                                                   op0=ALU.mult, op1=ALU.subtract).then_inc(s_lo, 1)

        @block.gpsimd
        def _(pool):
            n = 0
            nc.gpsimd.memset(zero[:], 0.0).then_inc(s_zero, 1)
            for ins in (nc.gpsimd.memset(ident[:], 0.0), nc.gpsimd.memset(ident16[:], 0.0), nc.gpsimd.memset(ident_big[:], 0.0),
                        nc.gpsimd.memset(causal[:], 0.0), nc.gpsimd.memset(lo_rows[:], 0.0), nc.gpsimd.memset(head_rows[:], 1.0),
                        nc.gpsimd.memset(neg_half[:], -0.5)):
                ins.then_inc(s_const, 1)
                n += 1
            pool.wait_ge(s_const, n)
            for m, one in ((ident, 1.0), (ident16, 1.0), (ident_big, 32768.0)):
                nc.gpsimd.affine_select(out=m[:], in_=m[:], compare_op=ALU.not_equal, fill=one, base=0,
                                        pattern=[[-1, P]], channel_multiplier=1).then_inc(s_const, 1)
            nc.gpsimd.affine_select(out=causal[:], in_=causal[:], compare_op=ALU.is_ge, fill=-65504.0, base=0,
                                    pattern=[[-1, P]], channel_multiplier=1).then_inc(s_const, 1)
            nc.gpsimd.affine_select(out=lo_rows[:], in_=lo_rows[:], compare_op=ALU.is_gt, fill=-1.0, base=HS,
                                    pattern=[[0, 1]], channel_multiplier=-1).then_inc(s_const, 1)
            nc.gpsimd.affine_select(out=head_rows[:], in_=head_rows[:], compare_op=ALU.is_ge, fill=0.0, base=0,
                                    pattern=[[-DK, HB], [0, CTX]], channel_multiplier=1).then_inc(s_const, 1)
            pool.wait_ge(s_const, n + 6)
            nc.gpsimd.affine_select(out=head_rows[:], in_=head_rows[:], compare_op=ALU.is_ge, fill=0.0, base=DK - 1,
                                    pattern=[[DK, HB], [0, CTX]], channel_multiplier=-1).then_inc(s_const, 1)

    x_t = sb("x_t", [P, 2, KC, P], F32)
    x_up = sb("x_up", [P, KC, P], F32)
    ctx_up = sb("ctx_up", [P, KC, CTX], F32)
    x2_up = sb("x2_up", [P, D], F32)
    x_nat = sb("x_nat", [P, 2, D], F32)
    x_hi = sb("x_hi", [P, 2, KC, P], F16)
    x_lo = sb("x_lo", [P, 2, KC, P], F16)
    q_hi = sb("q_hi", [P, 2, 4, P], F16)
    q_st = sb("q_st", [P, 2, P, H], F16)
    k_hi = sb("k_hi", [P, 2, P, H], F16)
    k_lo = sb("k_lo", [P, 2, P, H], F16)
    v_tok = sb("v_tok", [P, 2, H, 2, HS], F16)
    v_pos = sb("v_pos", [P, 2, 2 * GROUPS, 2, HS], F16)
    nmax = sb("nmax", [P, 2], F32)
    nbias = sb("nbias", [P, 2], F32)
    probs = sb("probs", [P, 384], F32)
    den = sb("den", [P, 2, 4], F32)
    rden = sb("rden", [P, 4], F32)
    pt_hi = sb("pt_hi", [P, 384], F16)
    pt_lo = sb("pt_lo", [P, 384], F16)
    o_norm = sb("o_norm", [P, 4, HS], F32)
    o_st = sb("o_st", [P, 2, 2 * GROUPS, 2, HS], F16)
    o_t = sb("o_t", [P, P, H], F16)
    y1 = sb("y1", [P, D], F32)
    y2 = sb("y2", [P, D], F32)
    stats = sb("stats", [P, 2, 6], F32)
    mv = sb("mv", [P, 2, 2], F32)
    var_eps = sb("var_eps", [P, 2], F32)
    rstd = sb("rstd", [P, 2], F32)
    x1 = sb("x1", [P, 2, D], F32)
    x1_hi = sb("x1_hi", [P, KC, P], F16)
    x1_lo = sb("x1_lo", [P, KC, P], F16)
    ctx_t = sb("ctx_t", [P, KC, CTX], F32)
    c_hi = sb("c_hi", [P, KC, CTX], F16)
    c_lo = sb("c_lo", [P, KC, CTX], F16)
    q2_hi = sb("q2_hi", [P, KC, P], F16)
    q2_lo = sb("q2_lo", [P, KC, P], F16)
    k2 = sb("k2", [P, 2, KC, CTX], F16)
    k2_bd = sb("k2_bd", [P, 2, KC, HB, CTX], F16)
    v2 = sb("v2", [CTX, 2, D], F16)
    sm = sb("sm", [P, 2, HB, CTX], F32)
    mx2 = sb("mx2", [P, HB], F32)
    sm_shift = sb("sm_shift", [P, HB, CTX], F32)
    probs2 = sb("probs2", [P, HB, CTX], F32)
    den2 = sb("den2", [P, 2, H], F32)
    rden2 = sb("rden2", [P, H], F32)
    pt2_hi = sb("pt2_hi", [CTX, HB, P], F16)
    pt2_lo = sb("pt2_lo", [CTX, HB, P], F16)
    o2_norm = sb("o2_norm", [P, H, DK], F32)
    o2_hi = sb("o2_hi", [P, KC, P], F16)
    o2_lo = sb("o2_lo", [P, KC, P], F16)
    x2 = sb("x2", [P, 2, D], F32)
    x2_pair = sb("x2_pair", [P, 2, 2, D], F16)
    x2_t = sb("x2_t", [P, KC, P], F32)
    logits = keep["logits"]
    piece = sb("piece", [P, PIECE], F32)
    piece_pair = sb("piece_pair", [P, 2, PIECE], F16)

    ps = ctx.enter_context(nc.psum_tensor("ps", [P, 8, 512], F32))
    ps_a = [ps[:, 0, :], ps[:, 1, :]]
    ps_s, ps_t, ps_o = ps[:, 2, :], ps[:, 3, :], ps[:, 4, :]
    c5, c6, c7 = ps[:, 5, :], ps[:, 6, :], ps[:, 7, :]

    (s_xt, s_xn, s_ctx, s_x_hi, s_x_lo, s_fill, s_fill_hi, s_fill_lo, s_v_out, s_v_in, s_scores, s_max, s_nbias,
     s_exp, s_pt, s_pt_hi, s_pt_lo, s_pv, s_rden, s_o_norm, s_o_hi, s_o_lo, s_ot, s_ot_a, s_ot_d, s_proj, s_y1,
     s_ln1, s_var1, s_rstd1, s_x1, s_x1t, s_x1_hi, s_x1_lo, s_c_hi, s_c_lo, s_q2, s_q2_hi, s_q2_lo, s_kv2, s_kv2_hi,
     s_kv2_lo, s_bd, s_s2, s_pred, s_mx2, s_shift, s_exp2, s_den2, s_t2, s_t2_hi, s_t2_lo, s_pv2, s_rden2, s_o2n,
     s_o2t, s_o2_hi, s_o2_lo, s_proj2, s_y2, s_ln2, s_var2, s_rstd2, s_x2, s_x2_hi, s_x2_lo, s_x2t, s_x2tc, s_lg,
     s_lgc, s_out_x2, s_out_pair, s_neg) = [sem("s1_%d_%s" % (n, m)) for n, m in enumerate(
        "xt xn ctx x_hi x_lo fill fill_hi fill_lo v_out v_in scores max nbias exp pt pt_hi pt_lo pv rden o_norm o_hi "
        "o_lo ot ot_a ot_d proj y1 ln1 var1 rstd1 x1 x1t x1_hi x1_lo c_hi c_lo q2 q2_hi q2_lo kv2 kv2_hi kv2_lo bd s2 "
        "pred mx2 shift exp2 den2 t2 t2_hi t2_lo pv2 rden2 o2n o2t o2_hi o2_lo proj2 y2 ln2 var2 rstd2 x2 x2_hi x2_lo "
        "x2t x2tc lg lgc out_x2 out_pair neg".split())]

    s_w_in, s_w_up, s_w_hi, s_w_lo, s_w_out = (sem("s1_" + n) for n in ("w_in", "w_up", "w_hi", "w_lo", "w_out"))
    s_xt, s_xn, s_out_x2, s_out_pair = ([s, sem("s1_odd_%d" % n)] for n, s in enumerate((s_xt, s_xn, s_out_x2, s_out_pair)))

    block = ctx.enter_context(nc.Block())

    def steps(eng, step):
        step(-1, 1, "A")
        step(0, 0, "AB")
        step(1, 1, "ABC")
        step(2, 0, "ABCD")
        step(3, 1, "ABCD")
        with eng.Fori(2, BATCH - 2, 1) as b:
            step(2 * b, 0, "ABCDW")
            step(2 * b + 1, 1, "ABCDW")
        step(TILES - 4, 0, "ABCD")
        step(TILES - 3, 1, "ABCD")
        step(TILES - 2, 0, "ABCD")
        step(TILES - 1, 1, "BCD")
        step(TILES, 0, "CD")
        step(TILES + 1, 1, "D")

    def since(t, n=0):
        return not (isinstance(t, int) and t < n)

    @block.sync
    def _(sp):
        def load_x(t, p):
            if since(t, 2):
                sp.wait_ge(s_x_lo, t - 1)
                sp.sem_inc(s_held_sp, 1)
            sp.dma_start(x_t[:, p], io["xT"].rearrange("(c p) n -> p c n", p=P)[:, :, bass.ds(t * P, P)]).then_inc(s_xt[p], 16)

        def step(s, p, stages):
            q = 1 - p
            if "W" in stages:
                n = s - 4
                sp.wait_ge(s_w_lo, n + 1)
                sp.sem_inc(s_held_sp, 1)
                sp.dma_start(piece[:], io["moe_w"][:, bass.ds(n * PIECE, PIECE)]).then_inc(s_w_in, 16)
            if isinstance(s, int) and s == -1:
                load_x(0, 0)
                load_x(1, 1)
            elif not (isinstance(s, int) and s + 2 >= TILES):
                load_x(s + 2, p)
            if "A" in stages:
                t = s + 1
                sp.wait_ge(s_fill_hi, NF * t + V_FILLS)
                sp.sem_inc(s_held_sp, 1)
                sp.wait_ge(s_fill_lo, NF * t + V_FILLS)
                sp.sem_inc(s_held_sp, 1)
                if since(t, 2):
                    sp.wait_ge(s_v_in, 16 * (t - 1))
                    sp.sem_inc(s_held_sp, 1)
                sp.dma_start(io["v_scr"][q], v_tok[:, q].rearrange("p h k d -> p (h k d)")).then_inc(s_v_out, 16)
                sp.wait_ge(s_v_out, 16 * (t + 1))
                sp.sem_inc(s_held_sp, 1)
                if since(t, 2):
                    sp.wait_ge(s_pv, GROUPS * (t - 1))
                    sp.sem_inc(s_held_sp, 1)
                sp.dma_start(v_pos[:, q].rearrange("p g k d -> p g (k d)"),
                             io["v_scr"][q].rearrange("(g t) (h e) -> (t h) g e", t=GTOK // 2, h=H)).then_inc(s_v_in, 16)
            if "B" in stages:
                t = s
                if since(t, 2):
                    sp.wait_ge(s_ln1, 3 * (t - 1))
                    sp.sem_inc(s_held_sp, 1)
                sp.dma_start(x_nat[:, p], io["x"][bass.ds(t * P, P), :]).then_inc(s_xn[p], 16)
                if p == 0:
                    if since(t, 2):
                        sp.wait_ge(s_c_lo, half(t))
                        sp.sem_inc(s_held_sp, 1)
                    sp.dma_start(ctx_t[:], io["ctxT"].rearrange("(c p) n -> p c n", p=P)[:, :, bass.ds(half(t) * CTX, CTX)]
                                 ).then_inc(s_ctx, 16)
            if "D" in stages:
                t = s - 2
                sp.wait_ge(s_x2, t + 1)
                sp.sem_inc(s_held_sp, 1)
                sp.dma_start(io["x2_scr"][bass.ds(t * P, P), :], x2[:, p]).then_inc(s_out_x2[p], 16)
                sp.wait_ge(s_x2_lo, t + 1)
                sp.sem_inc(s_held_sp, 1)
                sp.dma_start(io["pair_scr"][bass.ds(t * P, P), :], x2_pair[:, p].rearrange("p k d -> p (k d)")).then_inc(s_out_pair[p], 16)

            if "W" in stages:
                sp.wait_ge(s_w_lo, n + 2)
                sp.sem_inc(s_held_sp, 1)
                sp.dma_start(io["w_scr"].rearrange("k p n -> p k n")[:, :, bass.ds(n * PIECE, PIECE)], piece_pair[:]).then_inc(s_w_out, 16)

        steps(sp, step)
        sp.wait_ge(s_w_out, 16 * (PIECES + 1))
        for p in range(2):
            sp.wait_ge(s_out_x2[p], 16 * BATCH)
            sp.wait_ge(s_out_pair[p], 16 * BATCH)

    @block.tensor
    def _(pe):
        mm = nc.tensor.matmul

        def fill(t, p, j):
            kind, n = FILLS[j]
            if j == 0:
                pe.wait_ge(s_x_lo, t + 1)
            if since(t, 1) or j >= 2:
                pe.wait_ge(s_fill_lo, NF * t + j - 1)
            bank = ps_a[j % 2]
            xs = (x_hi[:, p], x_lo[:, p])
            if kind == "v":
                steps_ = [(a, b, c) for c in range(KC) for a, b in ((0, 0), (0, 1), (1, 0))]
                for m, (a, b, c) in enumerate(steps_):
                    last = mm(bank, xs[a][:, c], wv[:, b, c, n * 512:(n + 1) * 512], start=(m == 0), stop=(m == 5))
            else:
                for hh in range(4):
                    h = 4 * n + hh
                    w = wqk[kind]
                    steps_ = [(a, b, c) for c in range(KC) for a, b in ((0, 0), (1, 0), (0, 1))]
                    for m, (a, b, c) in enumerate(steps_):
                        last = mm(bank[:, hh * P:(hh + 1) * P], w[:, b, c, h].rearrange("p k d -> p (k d)"), xs[a][:, c],
                                  start=(m == 0), stop=(m == 5))
            last.then_inc(s_fill, 1)

        def scores(t, p, g):
            if g == 0:
                pe.wait_ge(s_fill_lo, NF * (t + 1))
            if since(t, 1) or g:
                pe.wait_ge(s_exp, 2 * (GROUPS * t + g))
            qs, kh, kl = (m[:, p, g * GTOK:(g + 1) * GTOK].rearrange("p t h -> p (t h)") for m in (q_st, k_hi, k_lo))
            mm(ps_s[:, 0:P], qs[:, 0:P], kh[:, 0:P], start=True, stop=False, skip_group_check=True)
            mm(ps_s[:, 0:P], qs[:, 0:P], kl[:, 0:P], start=False, stop=False, skip_group_check=True)
            mm(ps_s[:, 0:P], ident_big[:], causal[:], start=False, stop=True, skip_group_check=True)
            mm(ps_s[:, P:384], qs[:, P:256], kh[:, :], start=False, stop=False, skip_group_check=True)
            mm(ps_s[:, P:384], qs[:, P:256], kl[:, :], start=False, stop=False, skip_group_check=True)
            mm(ps_s[:, 256:384], ident_big[:], causal[:], start=False, stop=True,
               skip_group_check=True).then_inc(s_scores, 1)

        def turn_probs(t, g):
            pe.wait_ge(s_exp, 2 * (GROUPS * t + g) + 2)
            if since(t, 1) or g:
                pe.wait_ge(s_pt_lo, GROUPS * t + g)
            for b in range(3):
                last = nc.tensor.transpose(ps_t[:, b * P:(b + 1) * P], probs[:, b * P:(b + 1) * P], ident[:])
            last.then_inc(s_pt, 1)

        def pv(t, p, g):
            pe.wait_ge(s_pt_lo, GROUPS * t + g + 1)
            if g == 0:
                pe.wait_ge(s_v_in, 16 * (t + 1))
            if g % 2 == 0 and (since(t, 1) or g):
                pe.wait_ge(s_o_norm, 4 * t + g // 2)
            for q in range(2):
                out = ps_o[:, (g % 2 * 2 + q) * HS:(g % 2 * 2 + q + 1) * HS]
                blocks = [(0, 0)] if q == 0 else [(1, 0), (2, 1)]
                todo = [(a, b, blk, c) for blk, c in blocks for a, b in ((pt_hi, 0), (pt_hi, 1), (pt_lo, 0))]
                for m, (a, b, blk, c) in enumerate(todo):
                    last = mm(out, a[:, blk * P:(blk + 1) * P], v_pos[:, p, 2 * g + c, b], start=(m == 0), stop=(m == len(todo) - 1))
            last.then_inc(s_pv, 1)

        def stage_c(t, p, g):
            if g == 0:
                pe.wait_ge(s_o_lo, 4 * (t + 1))
                if since(t, 1):
                    pe.wait_ge(s_t2_lo, 4 * t)
                for half_, bank in enumerate((c5, c6)):
                    b16 = bank.bitcast(F16)
                    for n in range(8):
                        last = nc.tensor.transpose(b16[:, n * P:(n + 1) * P], o_st[:, p, 8 * half_ + n].rearrange("p k d -> p (k d)"), ident16[:])
                    last.then_inc(s_ot, 1)
            if g == 1:
                pe.wait_ge(s_ot_a, t + 1)
                pe.wait_ge(s_ot_d, t + 1)
                for h in range(H):
                    for k in range(2):
                        last = mm(c5[:, 0:D], o_t[:, :, h], wp[:, k, h], start=(h == 0 and k == 0), stop=(h == H - 1 and k == 1))
                last.then_inc(s_proj, 1)
            if g == 2:
                pe.wait_ge(s_x1, t + 1)
                for c in range(KC):
                    last = nc.tensor.transpose(c6[:, c * P:(c + 1) * P], x1[:, p, c * P:(c + 1) * P], ident[:])
                last.then_inc(s_x1t, 1)
            if g == 3:
                pe.wait_ge(s_x1_lo, t + 1)
                pe.wait_ge(s_y1, t + 1)
                for o in range(KC):
                    todo = [(a, b, c) for c in range(KC) for a, b in ((0, 0), (1, 0), (0, 1))]
                    for m, (a, b, c) in enumerate(todo):
                        last = mm(c5[:, o * P:(o + 1) * P], w2["q"][:, b, c, o * P:(o + 1) * P], (x1_hi, x1_lo)[a][:, c],
                                  start=(m == 0), stop=(m == 5))
                last.then_inc(s_q2, 1)
                if p == 0:
                    pe.wait_ge(s_c_lo, half(t) + 1)
                    for o in range(KC):
                        todo = [(a, b, c) for c in range(KC) for a, b in ((0, 0), (1, 0), (0, 1))]
                        for m, (a, b, c) in enumerate(todo):
                            mm(c6[:, o * CTX:(o + 1) * CTX], w2["k"][:, b, c, o * P:(o + 1) * P], (c_hi, c_lo)[a][:, c],
                               start=(m == 0), stop=(m == 5))
                    for m, (a, b, c) in enumerate(todo):
                        last = mm(c6[0:CTX, 256:512], (c_hi, c_lo)[a][:, c], w2["v"][:, b, c], start=(m == 0), stop=(m == 5))
                    last.then_inc(s_kv2, 1)
            if g in (4, 6):
                cc = (g - 4) // 2
                if cc == 1:
                    pe.wait_ge(s_t2_lo, 4 * t + 2)
                    pv2(t, 0)
                else:
                    pe.wait_ge(s_q2_lo, t + 1)
                    pe.wait_ge(s_bd, 4 * (half(t) + 1))
                for j, bank in enumerate((c5, c6)):
                    out = bank[:, 0:4 * CTX]
                    for m, (a, b) in enumerate(((q2_hi, 0), (q2_lo, 0), (q2_hi, 1))):
                        last = mm(out, a[:, cc], k2_bd[:, b, cc, 4 * j:4 * j + 4].rearrange("p h k -> p (h k)"), start=(m == 0), stop=(m == 2))
                last.then_inc(s_s2, 1)
            if g in (5, 7):
                cc = (g - 5) // 2
                pe.wait_ge(s_exp2, 2 * t + cc + 1)
                pe.wait_ge(s_pred, 4 * t + 2 * cc + 2)
                for j, bank in enumerate((c5, c6)):
                    for n in range(4):
                        last = nc.tensor.transpose(bank[0:CTX, n * P:(n + 1) * P], probs2[:, 4 * j + n], ident[:])
                    last.then_inc(s_t2, 1)

        def pv2(t, cc):
            if cc == 0 and since(t, 1):
                pe.wait_ge(s_lgc, t)
            for n in range(HB):
                h = HB * cc + n
                for m, (a, b) in enumerate(((pt2_hi, 0), (pt2_lo, 0), (pt2_hi, 1))):
                    last = mm(c7[:, h * DK:(h + 1) * DK], a[:, n], v2[:, b, h * DK:(h + 1) * DK], start=(m == 0), stop=(m == 2))
            last.then_inc(s_pv2, 1)

        def stage_d(t, p, g):
            if g == 0:
                pe.wait_ge(s_t2_lo, 4 * t + 4)
                pv2(t, 1)
            if g == 1:
                pe.wait_ge(s_o2n, t + 1)
                o = o2_norm[:].rearrange("p h d -> p (h d)")
                for c in range(KC):
                    last = nc.tensor.transpose(c7[:, c * P:(c + 1) * P], o[:, c * P:(c + 1) * P], ident[:])
                last.then_inc(s_o2t, 1)
            if g == 2:
                pe.wait_ge(s_o2_lo, t + 1)
                todo = [(a, b, c) for c in range(KC) for a, b in ((0, 0), (1, 0), (0, 1))]
                for m, (a, b, c) in enumerate(todo):
                    last = mm(c7[:, 0:D], (o2_hi, o2_lo)[a][:, c], w2["o"][:, b, c], start=(m == 0), stop=(m == 5))
                last.then_inc(s_proj2, 1)
            if g == 3:
                pe.wait_ge(s_x2, t + 1)
                for c in range(KC):
                    last = nc.tensor.transpose(c7[:, c * P:(c + 1) * P], x2[:, p, c * P:(c + 1) * P], ident[:])
                last.then_inc(s_x2t, 1)
            if g == 4:
                pe.wait_ge(s_x2tc, t + 1)
                for c in range(KC):
                    last = mm(c7[:, 0:E], x2_t[:, c], wr[:, c], start=(c == 0), stop=(c == KC - 1))
                last.then_inc(s_lg, 1)

        def step(s, p, stages):
            for g in range(GROUPS):
                if "B" in stages:
                    scores(s, p, g)
                if "A" in stages:
                    for j in FILLS_OF_SLOT[g]:
                        fill(s + 1, 1 - p, j)
                if "B" in stages:
                    turn_probs(s, g)
                if "D" in stages:
                    stage_d(s - 2, p, g)
                if "C" in stages:
                    stage_c(s - 1, 1 - p, g)
                if "B" in stages:
                    pv(s, p, g)

        steps(pe, step)

    @block.scalar
    def _(act):
        def hi(t, p, j):
            kind, n = FILLS[j]
            act.wait_ge(s_fill, NF * t + j + 1)
            if j == 0 and since(t, 2):
                act.wait_ge(s_v_out, 16 * (t - 1))
                act.wait_ge(s_scores, GROUPS * (t - 1))
            if kind == "v":
                src = ps_a[j % 2].rearrange("p (h d) -> p h d", d=HS)
                dst = v_tok[:, p, 8 * n:8 * n + 8, 0]
            elif kind == "q":
                if since(t, 1) or j >= 3:
                    act.wait_ge(s_fill_lo, NF * t + j - 1)
                src = ps_a[j % 2].rearrange("p (h t) -> p h t", h=4)
                dst = q_hi[:, j % 2]
            else:
                src = ps_a[j % 2].rearrange("p (h t) -> p h t", h=4)
                dst = k_hi[:, p, :, 4 * n:4 * n + 4].rearrange("p t h -> p h t")
            nc.scalar.activation(dst, src, ACT.Copy).then_inc(s_fill_hi, 1)

        def exps(t, g):
            act.wait_ge(s_nbias, GROUPS * t + g + 1)
            for q, (lo_, up_) in enumerate(((0, P), (P, 384))):
                nc.scalar.activation(probs[:, lo_:up_], ps_s[:, lo_:up_], ACT.Exp, bias=nbias[:, q:q + 1], scale=SCORE_SCALE,
                                     accum_out=den[:, g // 2 % 2, g % 2 * 2 + q:g % 2 * 2 + q + 1]).then_inc(s_exp, 1)

        def pt(t, g):
            act.wait_ge(s_pt, GROUPS * t + g + 1)
            nc.scalar.activation(pt_hi[:], ps_t[:, 0:384], ACT.Copy).then_inc(s_pt_hi, 1)

        def exp2(t, cc):
            act.wait_ge(s_shift, 2 * t + cc + 1)
            nc.scalar.activation(probs2[:], sm_shift[:], ACT.Exp, scale=SCORE2_SCALE).then_inc(s_exp2, 1)

        def stage_c(t, p, g):
            if g == 0:
                act.wait_ge(s_ot, 2 * t + 1)
                nc.scalar.activation(o_t[:, 0:64].rearrange("p t h -> p (t h)"), c5.bitcast(F16), ACT.Copy).then_inc(s_ot_a, 1)
            if g == 2:
                act.wait_ge(s_x1t, t + 1)
                nc.scalar.activation(x1_hi[:].rearrange("p c t -> p (c t)"), c6[:, 0:D], ACT.Copy, scale=X_UP).then_inc(s_x1_hi, 1)
            if g == 3:
                act.wait_ge(s_q2, t + 1)
                nc.scalar.activation(q2_hi[:].rearrange("p c t -> p (c t)"), c5[:, 0:D], ACT.Copy).then_inc(s_q2_hi, 1)
                if p == 0:
                    act.wait_ge(s_kv2, half(t) + 1)
                    if since(t, 2):
                        act.wait_ge(s_bd, 4 * half(t))
                    nc.scalar.activation(k2[:, 0], c6[:, 0:KC * CTX].rearrange("p (c k) -> p c k", c=KC), ACT.Copy).then_inc(s_kv2_hi, 1)
                    nc.scalar.activation(v2[:, 0], c6[0:CTX, 256:512], ACT.Copy).then_inc(s_kv2_hi, 1)
            if g in (5, 7):
                cc = (g - 5) // 2
                for j, bank in enumerate((c5, c6)):
                    act.wait_ge(s_t2, 4 * t + 2 * cc + j + 1)
                    nc.scalar.activation(pt2_hi[:, 4 * j:4 * j + 4].rearrange("p h t -> p (h t)"), bank[0:CTX, :], ACT.Copy).then_inc(s_t2_hi, 1)

        def stage_d(t, p, g):
            if g == 1:
                act.wait_ge(s_o2t, t + 1)
                nc.scalar.activation(o2_hi[:].rearrange("p c t -> p (c t)"), c7[:, 0:D], ACT.Copy).then_inc(s_o2_hi, 1)
            if g == 3:
                act.wait_ge(s_x2t, t + 1)
                nc.scalar.activation(x2_t[:].rearrange("p c t -> p (c t)"), c7[:, 0:D], ACT.Copy).then_inc(s_x2tc, 1)

        def step(s, p, stages):
            for g in range(GROUPS):
                if "C" in stages and g in (5, 7):
                    exp2(s - 1, (g - 5) // 2)
                if "B" in stages:
                    exps(s, g)
                if "A" in stages:
                    for j in FILLS_OF_SLOT[g]:
                        hi(s + 1, 1 - p, j)
                if "B" in stages:
                    pt(s, g)
                if "D" in stages:
                    stage_d(s - 2, p, g)
                if "C" in stages:
                    stage_c(s - 1, 1 - p, g)

        steps(act, step)

    @block.vector
    def _(dve):
        stt = nc.vector.scalar_tensor_tensor

        def lo(t, p, j):
            kind, n = FILLS[j]
            dve.wait_ge(s_fill_hi, NF * t + j + 1)
            if kind == "v":
                src = ps_a[j % 2].rearrange("p (h d) -> p h d", d=HS)
                stt(out=v_tok[:, p, 8 * n:8 * n + 8, 1], in0=src, scalar=1.0, in1=v_tok[:, p, 8 * n:8 * n + 8, 0],
                    op0=ALU.mult, op1=ALU.subtract).then_inc(s_fill_lo, 1)
            elif kind == "q":
                src = ps_a[j % 2].rearrange("p (h t) -> p h t", h=4)
                stt(out=q_st[:, p, :, 4 * n:4 * n + 4].rearrange("p t h -> p h t"), in0=q_hi[:, j % 2], scalar=lo_rows[:, 0:1],
                    in1=src, op0=ALU.mult, op1=ALU.add).then_inc(s_fill_lo, 1)
            else:
                src = ps_a[j % 2].rearrange("p (h t) -> p h t", h=4)
                at = (slice(None), p, slice(None), slice(4 * n, 4 * n + 4))
                stt(out=k_lo[at].rearrange("p t h -> p h t"), in0=src, scalar=1.0, in1=k_hi[at].rearrange("p t h -> p h t"),
                    op0=ALU.mult, op1=ALU.subtract).then_inc(s_fill_lo, 1)

        def maxima(t, g):
            n = GROUPS * t + g
            dve.wait_ge(s_scores, n + 1)
            for q, (lo_, up_) in enumerate(((0, P), (P, 384))):
                nc.vector.tensor_reduce(nmax[:, q:q + 1], ps_s[:, lo_:up_], AX.X, ALU.max).then_inc(s_max, 1)
            dve.wait_ge(s_max, 2 * n + 2)
            nc.vector.tensor_scalar(nbias[:], nmax[:], -SCORE_SCALE, None, ALU.mult).then_inc(s_nbias, 1)

        def pt(t, g):
            dve.wait_ge(s_pt_hi, GROUPS * t + g + 1)
            nc.vector.tensor_tensor(pt_lo[:], ps_t[:, 0:384], pt_hi[:], ALU.subtract).then_inc(s_pt_lo, 1)

        def normalise(t, g):
            pair = 4 * t + g // 2
            nc.vector.reciprocal(rden[:], den[:, g // 2 % 2]).then_inc(s_rden, 1)
            dve.wait_ge(s_rden, pair + 1)
            dve.wait_ge(s_pv, 2 * pair + 2)
            if since(t, 1) or g > 1:
                dve.wait_ge(s_o_lo, pair)
            nc.vector.tensor_tensor(o_norm[:], ps_o[:, 0:4 * HS].rearrange("p (q d) -> p q d", d=HS),
                                    rden[:].unsqueeze(2).to_broadcast([P, 4, HS]), ALU.mult).then_inc(s_o_norm, 1)

        def moments(t, ln, y, s_ln, s_var):
            dve.wait_ge(s_ln, 3 * t + 1)
            nc.vector.bn_stats(stats[:, ln], y[:]).then_inc(s_ln, 1)
            dve.wait_ge(s_ln, 3 * t + 2)
            dve.sem_inc(s_held_dve, 1)
            nc.vector.bn_aggr(mv[:, ln], stats[:, ln]).then_inc(s_ln, 1)
            dve.wait_ge(s_ln, 3 * t + 3)
            nc.vector.tensor_scalar(var_eps[:, ln:ln + 1], mv[:, ln, 1:2], EPS, None, ALU.add).then_inc(s_var, 1)

        def predicated(t, p, cc):
            dve.wait_ge(s_s2, 2 * t + cc + 1)
            dve.sem_inc(s_held_dve, 1)
            for j, bank in enumerate((c5, c6)):
                nc.vector.copy_predicated(sm[:, p, 4 * j:4 * j + 4], mask[:, p].unsqueeze(1).to_broadcast([P, 4, CTX]),
                                          bank[:, 0:4 * CTX].rearrange("p (h k) -> p h k", h=4)).then_inc(s_pred, 1)
            dve.wait_ge(s_pred, 4 * t + 2 * cc + 2)
            if since(t, 1) or cc:
                dve.wait_ge(s_shift, 2 * t + cc)
            nc.vector.tensor_reduce(mx2[:], sm[:, p], AX.X, ALU.max).then_inc(s_mx2, 1)

        def start(t, p, g):
            if g == 2:
                dve.wait_ge(s_rstd1, t + 1)
                nc.vector.tensor_scalar(x1[:, p], y1[:], mv[:, 0, 0:1], rstd[:, 0:1], ALU.subtract, ALU.mult).then_inc(s_x1, 1)

        def stage_c(t, p, g):
            if g == 0:
                dve.wait_ge(s_ot, 2 * t + 2)
                nc.vector.tensor_copy(o_t[:, 64:128].rearrange("p t h -> p (t h)"), c6.bitcast(F16)).then_inc(s_ot_d, 1)
            if g == 1:
                dve.wait_ge(s_proj, t + 1)
                dve.wait_ge(s_xn[p], 16 * (half(t) + 1))
                stt(out=y1[:], in0=c5[:, 0:D], scalar=1.0 / (QK_UP * WP_UP), in1=x_nat[:, p], op0=ALU.mult,
                    op1=ALU.add).then_inc(s_y1, 1)
                dve.wait_ge(s_y1, t + 1)
                nc.vector.tensor_tensor(y1[:], y1[:], proj_b[:], ALU.add).then_inc(s_ln1, 1)
                moments(t, 0, y1, s_ln1, s_var1)
            if g == 2:
                dve.wait_ge(s_x1_hi, t + 1)
                stt(out=x1_lo[:].rearrange("p c t -> p (c t)"), in0=c6[:, 0:D], scalar=X_UP,
                    in1=x1_hi[:].rearrange("p c t -> p (c t)"), op0=ALU.mult, op1=ALU.subtract).then_inc(s_x1_lo, 1)
            if g == 3:
                dve.wait_ge(s_q2_hi, t + 1)
                nc.vector.tensor_tensor(q2_lo[:].rearrange("p c t -> p (c t)"), c5[:, 0:D],
                                        q2_hi[:].rearrange("p c t -> p (c t)"), ALU.subtract).then_inc(s_q2_lo, 1)
                if p == 0:
                    dve.wait_ge(s_kv2_hi, 2 * (half(t) + 1))
                    nc.vector.tensor_tensor(k2[:, 1], c6[:, 0:KC * CTX].rearrange("p (c k) -> p c k", c=KC), k2[:, 0],
                                            ALU.subtract).then_inc(s_kv2_lo, 1)
                    nc.vector.tensor_tensor(v2[:, 1], c6[0:CTX, 256:512], v2[:, 0], ALU.subtract).then_inc(s_kv2_lo, 1)
            if g in (4, 6):
                predicated(t, p, (g - 4) // 2)
            if g in (5, 7):
                cc = (g - 5) // 2
                dve.wait_ge(s_exp2, 2 * t + cc + 1)
                nc.vector.tensor_reduce(den2[:, p, cc * HB:(cc + 1) * HB], probs2[:], AX.X, ALU.add).then_inc(s_den2, 1)
                for j, bank in enumerate((c5, c6)):
                    dve.wait_ge(s_t2_hi, 4 * t + 2 * cc + j + 1)
                    at = pt2_hi[:, 4 * j:4 * j + 4].rearrange("p h t -> p (h t)")
                    nc.vector.tensor_tensor(pt2_lo[:, 4 * j:4 * j + 4].rearrange("p h t -> p (h t)"), bank[0:CTX, :], at,
                                            ALU.subtract).then_inc(s_t2_lo, 1)

        def stage_d(t, p, g):
            if g == 0:
                dve.wait_ge(s_den2, 2 * t + 2)
                nc.vector.reciprocal(rden2[:], den2[:, p]).then_inc(s_rden2, 1)
                dve.wait_ge(s_rden2, t + 1)
                dve.wait_ge(s_pv2, 2 * t + 2)
                nc.vector.tensor_tensor(o2_norm[:], c7[:, 0:D].rearrange("p (h d) -> p h d", d=DK),
                                        rden2[:].unsqueeze(2).to_broadcast([P, H, DK]), ALU.mult).then_inc(s_o2n, 1)
            if g == 1:
                dve.wait_ge(s_o2_hi, t + 1)
                nc.vector.tensor_tensor(o2_lo[:].rearrange("p c t -> p (c t)"), c7[:, 0:D],
                                        o2_hi[:].rearrange("p c t -> p (c t)"), ALU.subtract).then_inc(s_o2_lo, 1)
            if g == 2:
                dve.wait_ge(s_proj2, t + 1)
                stt(out=y2[:], in0=c7[:, 0:D], scalar=1.0 / (QK_UP * WA_UP), in1=x1[:, p], op0=ALU.mult,
                    op1=ALU.add).then_inc(s_ln2, 1)
                moments(t, 1, y2, s_ln2, s_var2)
            if g == 4:
                dve.wait_ge(s_lg, t + 1)
                nc.vector.tensor_copy(logits[:, bass.ds(t * E, E)], c7[:, 0:E]).then_inc(s_lgc, 1)

        def start_d(t, p, g):
            if g == 3:
                dve.wait_ge(s_rstd2, t + 1)
                if since(t, 2):
                    dve.wait_ge(s_out_x2[p], 16 * half(t))
                    dve.wait_ge(s_x2_lo, t - 1)
                nc.vector.tensor_scalar(x2[:, p], y2[:], mv[:, 1, 0:1], rstd[:, 1:2], ALU.subtract, ALU.mult).then_inc(s_x2, 1)

        def step(s, p, stages):
            for g in range(GROUPS):
                if "C" in stages:
                    start(s - 1, 1 - p, g)
                if "D" in stages:
                    start_d(s - 2, p, g)
                if "B" in stages:
                    maxima(s, g)
                if "A" in stages:
                    for j in FILLS_OF_SLOT[g]:
                        lo(s + 1, 1 - p, j)
                if "B" in stages:
                    pt(s, g)
                if "D" in stages:
                    stage_d(s - 2, p, g)
                if "C" in stages:
                    stage_c(s - 1, 1 - p, g)
                if "B" in stages and g % 2:
                    normalise(s, g)

        nc.vector.memset(sm[:], NEG2).then_inc(s_neg, 1)
        dve.wait_ge(s_neg, 1)
        steps(dve, step)

    @block.gpsimd
    def _(pool):
        def split(pool, src, up, hi, lo, n, s_hi, s_lo):
            if since(n, 1):
                pool.wait_ge(s_lo, n)
            pool.sem_inc(s_held_pool, 1)
            nc.gpsimd.tensor_scalar(up, src, X_UP, None, ALU.mult).then_inc(s_hi, 1)
            pool.wait_ge(s_hi, 2 * n + 1)
            pool.sem_inc(s_held_pool, 1)
            nc.gpsimd.tensor_copy(hi, up).then_inc(s_hi, 1)
            pool.wait_ge(s_hi, 2 * n + 2)
            nc.gpsimd.tensor_tensor(lo, up, hi, ALU.subtract).then_inc(s_lo, 1)

        def split_x(t, p):
            pool.wait_ge(s_xt[p], 16 * (half(t) + 1))
            if since(t, 2):
                pool.wait_ge(s_fill, NF * (t - 1))
            split(pool, x_t[:, p], x_up[:], x_hi[:, p], x_lo[:, p], t, s_x_hi, s_x_lo)

        def split_o(t, p, g):
            pair = 4 * t + g // 2
            pool.wait_ge(s_o_norm, pair + 1)
            if g == 1 and since(t, 2):
                pool.wait_ge(s_ot, 2 * (t - 1))
            at = o_st[:, p, 2 * (g - 1):2 * (g + 1)]
            pool.sem_inc(s_held_pool, 1)
            nc.gpsimd.tensor_copy(at[:, :, 0], o_norm[:]).then_inc(s_o_hi, 1)
            pool.wait_ge(s_o_hi, pair + 1)
            nc.gpsimd.tensor_tensor(at[:, :, 1], o_norm[:], at[:, :, 0], ALU.subtract).then_inc(s_o_lo, 1)

        def step(s, p, stages):
            if isinstance(s, int) and s == -1:
                pool.sem_inc(s_w_out, 16)
                pool.sem_inc(s_w_lo, 1)
                split_x(0, 0)
                split_x(1, 1)
            for g in range(GROUPS):
                if "W" in stages and g in (4, 5, 6):
                    n = s - 4
                    if g == 4:
                        pool.wait_ge(s_w_in, 16 * (n + 1))
                        pool.sem_inc(s_held_pool, 1)
                        nc.gpsimd.tensor_scalar(piece[:], piece[:], WP_UP, None, ALU.mult).then_inc(s_w_up, 1)
                    if g == 5:
                        pool.wait_ge(s_w_up, n + 1)
                        pool.wait_ge(s_w_out, 16 * (n + 1))
                        pool.sem_inc(s_held_pool, 1)
                        nc.gpsimd.tensor_copy(piece_pair[:, 0], piece[:]).then_inc(s_w_hi, 1)
                    if g == 6:
                        pool.wait_ge(s_w_hi, n + 1)
                        nc.gpsimd.tensor_tensor(piece_pair[:, 1], piece[:], piece_pair[:, 0], ALU.subtract).then_inc(s_w_lo, 1)
                if g == 2 and not isinstance(s, int) or g == 2 and isinstance(s, int) and 0 <= s < TILES - 2:
                    split_x(s + 2, p)
                if "D" in stages and g == 2:
                    pool.wait_ge(s_var2, s - 1)
                    nc.gpsimd.tensor_tensor(rstd[:, 1:2], var_eps[:, 1:2], neg_half[:], ALU.pow).then_inc(s_rstd2, 1)
                if "D" in stages and g == 3:
                    t = s - 2
                    pool.wait_ge(s_x2, t + 1)
                    if since(t, 2):
                        pool.wait_ge(s_out_pair[p], 16 * half(t))
                    split(pool, x2[:, p], x2_up[:], x2_pair[:, p, 0], x2_pair[:, p, 1], t, s_x2_hi, s_x2_lo)
                if "C" in stages:
                    t = s - 1
                    if g == 1:
                        pool.wait_ge(s_var1, t + 1)
                        nc.gpsimd.tensor_tensor(rstd[:, 0:1], var_eps[:, 0:1], neg_half[:], ALU.pow).then_inc(s_rstd1, 1)
                        if p == 1:
                            pool.wait_ge(s_ctx, 16 * (half(t) + 1))
                            if since(t, 2):
                                pool.wait_ge(s_kv2, half(t))
                            split(pool, ctx_t[:], ctx_up[:], c_hi[:], c_lo[:], half(t), s_c_hi, s_c_lo)
                    if g == 3 and p == 1:
                        pool.wait_ge(s_kv2_lo, 2 * (half(t) + 1))
                        for k in range(2):
                            for c in range(KC):
                                nc.gpsimd.tensor_tensor(k2_bd[:, k, c], head_rows[:], k2[:, k, c].unsqueeze(1).to_broadcast([P, HB, CTX]),
                                                        ALU.mult).then_inc(s_bd, 1)
                    if g in (4, 6):
                        cc = (g - 4) // 2
                        pool.wait_ge(s_mx2, 2 * t + cc + 1)
                        if since(t, 1) or cc:
                            pool.wait_ge(s_exp2, 2 * t + cc)
                        nc.gpsimd.tensor_tensor(sm_shift[:], sm[:, 1 - p], mx2[:].unsqueeze(2).to_broadcast([P, HB, CTX]),
                                                ALU.subtract).then_inc(s_shift, 1)
                if "B" in stages and g % 2:
                    split_o(s, p, g)

        steps(pool, step)


def half(t):
    return t >> 1


SLOT_TILES = (2 * TOKENS + NE * (P - 1)) // P
CODES = 2 * TOKENS
H_UP = X_UP * WP_UP
G_UP = 16.0


def routing_block(nc, ctx, io, keep):
    def sb(name, shape, dt):
        return ctx.enter_context(nc.sbuf_tensor(name, shape, dt))

    def sem(name):
        return ctx.enter_context(nc.semaphore(name))

    T = TILES
    logits = keep["logits"]
    lg = logits[:].rearrange("p (t e) -> p t e", e=E)
    ps = ctx.enter_context(nc.psum_tensor("ps_r", [P, 4, 512], F32))
    tri = sb("tri", [P, P], F16)
    ones = sb("ones", [P, P], F16)
    iota_e = sb("iota_e", [P, E], F32)
    iota_lo = sb("iota_lo", [P, P], F32)
    iota_hi = sb("iota_hi", [P, SLOT_TILES], F32)
    iota_hi1 = sb("iota_hi1", [P, SLOT_TILES], F32)
    codes = sb("codes", [P, 2, T], F32)
    one_row = sb("one_row", [P, T], F32)
    mx = sb("r_mx", [P, T], F32)
    ex = sb("r_ex", [P, T, E], F32)
    sm = sb("r_sm", [P, T], F32)
    pr = sb("r_pr", [P, T, E], F32)
    m = sb("r_m", [P, 2, T], F32)
    tmp = sb("r_tmp", [P, T, E], F32)
    ix = sb("r_ix", [P, 2, T], F32)
    hot = sb("r_hot", [P, 2, T, E], F32)
    both = sb("r_both", [P, E, T], F32)
    elig = sb("r_elig", [P, NE, T], F32)
    elig16 = sb("r_elig16", [P, NE, T], F16)
    free = sb("r_free", [P, T], F32)
    cum = sb("r_cum", [P, NE, T], F32)
    pos = sb("r_pos", [P, NE, T], F32)
    kept = sb("r_kept", [P, NE, T], F32)
    over = sb("r_over", [P, E, T], F32)
    cnt = sb("r_cnt", [P, NE], F32)
    cnt_i = sb("r_cnt_i", [P, NE], I32)
    tiles = sb("r_tiles", [P, NE], F32)
    cumt = sb("r_cumt", [P, NE], F32)
    base = sb("r_base", [P, NE], F32)
    slot = sb("r_slot", [P, NE, T], F32)
    sk = sb("r_sk", [P, 2, T], F32)
    ovk = sb("r_ovk", [P, 2, T], F32)
    w = keep["weights"]
    tot = sb("r_tot", [P, T], F32)
    si = sb("r_si", [P, 2, T], I32)
    hi_i = sb("r_hi_i", [P, 2, T], I32)
    lo_i = sb("r_lo_i", [P, 2, T], I32)
    hi_f = sb("r_hi_f", [P, 2, T], F32)
    lo_f = sb("r_lo_f", [P, 2, T], F32)
    RING = 8
    ring_lo = sb("ring_lo", [P, RING, P], F32)
    ring_hi = sb("ring_hi", [P, RING, SLOT_TILES], F32)
    code = sb("r_code", [P, SLOT_TILES], F32)
    pad = sb("r_pad", [P, SLOT_TILES], F32)
    tokf = sb("r_tokf", [P, SLOT_TILES], F32)
    te = sb("r_te", [P, SLOT_TILES], F32)
    tok_i, dst_i, te_i = keep["tok_i"], keep["dst_i"], keep["te_i"]

    s_const = sem("r_const")
    s_tri = sem("r_tri")
    s_ch = sem("r_chain")
    s_shift = sem("r_shifted")
    s_exp = sem("r_exped")
    s_elig = sem("r_elig_ready")
    s_pref = sem("r_prefixes")
    s_pref_used = sem("r_prefixes_used")
    s_hot = sem("r_hot_ready")
    s_place = sem("r_placed")
    s_w = keep["s_w"]
    block = ctx.enter_context(nc.Block())

    @block.sync
    def _(sp):
        for e in range(NE):
            for k in range(2):
                sp.dma_start(keep["wres"][:, k, e * WSIZE:(e + 1) * WSIZE], io["w_scr"][k, :, e * WSIZE:(e + 1) * WSIZE]).then_inc(s_w[e], 16)
        sp.dma_start(keep["b1"][:], io["b1T"]).then_inc(keep["s_b"], 16)
        sp.dma_start(keep["b2"][:], io["b2"].rearrange("(a n) -> a n", a=1).partition_broadcast(P)[:, 0, :]).then_inc(keep["s_b"], 16)

    @block.gpsimd
    def _(pool):
        g = nc.gpsimd
        g.memset(tri[:], 1.0).then_inc(s_tri, 1)
        g.memset(ones[:], 1.0).then_inc(s_const, 1)
        g.memset(one_row[:], 1.0).then_inc(s_const, 1)
        big = dict(allow_small_or_imprecise_dtypes=True)
        g.iota(iota_e[:], pattern=[[1, E]], base=0, channel_multiplier=0, **big).then_inc(s_const, 1)
        g.iota(iota_lo[:], pattern=[[1, P]], base=0, channel_multiplier=0, **big).then_inc(s_const, 1)
        g.iota(iota_hi[:], pattern=[[1, SLOT_TILES]], base=0, channel_multiplier=0, **big).then_inc(s_const, 1)
        g.iota(iota_hi1[:], pattern=[[1, SLOT_TILES]], base=1, channel_multiplier=0, **big).then_inc(s_const, 1)
        g.iota(codes[:], pattern=[[1, 2], [2 * P, T]], base=1, channel_multiplier=2, **big).then_inc(s_const, 1)
        pool.wait_ge(s_tri, 1)
        g.affine_select(out=tri[:], in_=tri[:], compare_op=ALU.is_ge, fill=0.0, base=0, pattern=[[1, P]],
                        channel_multiplier=-1).then_inc(s_const, 1)

    @block.scalar
    def _(act):
        act.wait_ge(s_shift, 1)
        nc.scalar.activation(ex[:].rearrange("p t e -> p (t e)"), pr[:].rearrange("p t e -> p (t e)"), ACT.Exp).then_inc(s_exp, 1)

    @block.tensor
    def _(pe):
        pe.wait_ge(s_const, 8)
        for e in range(NE):
            pe.wait_ge(s_elig, e + 1)
            if e:
                pe.wait_ge(s_pref_used, e)
            nc.tensor.matmul(ps[:, 0, 0:T], tri[:], elig16[:, e], start=True, stop=True)
            nc.tensor.matmul(ps[:, 0, T:2 * T], ones[:], elig16[:, e], start=True, stop=True).then_inc(s_pref, 1)
        for n in range(2 * T):
            pe.wait_ge(s_hot, 2 * n + 2)
            nc.tensor.matmul(ps[:, 1, 0:SLOT_TILES], ring_lo[:, n % RING], ring_hi[:, n % RING], start=(n == 0),
                             stop=(n == 2 * T - 1)).then_inc(s_place, 1)

    @block.vector
    def _(dve):
        v = nc.vector
        done = [0]

        def link(ins):
            done[0] += 1
            ins.then_inc(s_ch, 1)
            dve.wait_ge(s_ch, done[0])

        def wide(a, n=E):
            return a.unsqueeze(2).to_broadcast([P, T, n])

        link(v.tensor_reduce(mx[:], lg, AX.X, ALU.max))
        v.tensor_tensor(pr[:], lg, wide(mx[:]), ALU.subtract).then_inc(s_shift, 1)
        dve.wait_ge(s_exp, 1)
        link(v.tensor_reduce(sm[:], ex[:], AX.X, ALU.add))
        link(v.reciprocal(mx[:], sm[:]))
        link(v.tensor_tensor(pr[:], ex[:], wide(mx[:]), ALU.mult))
        dve.wait_ge(s_const, 8)
        ie = iota_e[:].unsqueeze(1).to_broadcast([P, T, E])
        for k in range(2):
            link(v.tensor_reduce(m[:, k], pr[:], AX.X, ALU.max))
            link(v.tensor_tensor(tmp[:], pr[:], wide(m[:, k]), ALU.is_lt))
            link(v.scalar_tensor_tensor(out=tmp[:], in0=tmp[:], scalar=100.0, in1=ie, op0=ALU.mult, op1=ALU.add))
            link(v.tensor_reduce(ix[:, k], tmp[:], AX.X, ALU.min))
            link(v.tensor_tensor(hot[:, k], ie, wide(ix[:, k]), ALU.is_equal))
            if k == 0:
                link(v.scalar_tensor_tensor(out=pr[:], in0=hot[:, 0], scalar=-4.0, in1=pr[:], op0=ALU.mult, op1=ALU.add))
        link(v.tensor_tensor(sm[:], m[:, 0], m[:, 1], ALU.add))
        link(v.tensor_scalar(sm[:], sm[:], 1e-9, None, ALU.max))
        link(v.reciprocal(mx[:], sm[:]))
        for k in range(2):
            link(v.tensor_tensor(w[:, k], m[:, k], mx[:], ALU.mult))
        link(v.tensor_tensor(both[:].rearrange("p e t -> p t e"), hot[:, 0], hot[:, 1], ALU.add))
        link(v.tensor_scalar(free[:], one_row[:], 1.0, None, ALU.mult))
        for e in range(NE):
            if e < E:
                link(v.tensor_tensor(elig[:, e], both[:, e], free[:], ALU.mult))
            else:
                link(v.tensor_scalar(elig[:, e], free[:], -1.0, 1.0, ALU.mult, ALU.add))
            v.tensor_copy(elig16[:, e], elig[:, e]).then_inc(s_elig, 1)
            dve.wait_ge(s_pref, e + 1)
            link(v.tensor_copy(tot[:], ps[:, 0, T:2 * T]))
            link(v.tensor_tensor_scan(cum[:, e], one_row[:], tot[:], 0.0, ALU.mult, ALU.add))
            link(v.tensor_tensor(pos[:, e], cum[:, e], tot[:], ALU.subtract))
            v.tensor_tensor(pos[:, e], pos[:, e], ps[:, 0, 0:T], ALU.add).then_inc(s_pref_used, 1)
            dve.wait_ge(s_pref_used, e + 1)
            if e < E:
                link(v.scalar_tensor_tensor(out=kept[:, e], in0=pos[:, e], scalar=float(CAP), in1=elig[:, e], op0=ALU.is_le, op1=ALU.mult))
                link(v.tensor_tensor(over[:, e], elig[:, e], kept[:, e], ALU.subtract))
                link(v.tensor_tensor(free[:], free[:], over[:, e], ALU.subtract))
                link(v.tensor_scalar(cnt[:, e:e + 1], cum[:, e, T - 1:T], float(CAP), None, ALU.min))
            else:
                link(v.tensor_scalar(cnt[:, e:e + 1], cum[:, e, T - 1:T], 1.0, None, ALU.mult))
        link(v.tensor_scalar(cnt[:], cnt[:], float(P - 1), None, ALU.add))
        link(v.tensor_copy(cnt_i[:], cnt[:]))
        link(v.tensor_single_scalar(cnt_i[:], cnt_i[:], 7, ALU.arith_shift_right))
        link(v.tensor_copy(tiles[:], cnt_i[:]))
        link(v.tensor_tensor_scan(cumt[:], one_row[:, 0:NE], tiles[:], 0.0, ALU.mult, ALU.add))
        link(v.tensor_tensor(base[:], cumt[:], tiles[:], ALU.subtract))
        link(v.tensor_scalar(base[:], base[:], float(P), None, ALU.mult))
        link(v.tensor_tensor(slot[:], pos[:], base[:].unsqueeze(2).to_broadcast([P, NE, T]), ALU.add))
        link(v.tensor_tensor(slot[:, 0:E], slot[:, 0:E], kept[:, 0:E], ALU.mult))
        for k in range(2):
            link(v.tensor_tensor(tmp[:], hot[:, k], slot[:, 0:E].rearrange("p e t -> p t e"), ALU.mult))
            link(v.tensor_reduce(sk[:, k], tmp[:], AX.X, ALU.add))
            link(v.tensor_tensor(tmp[:], hot[:, k], over[:].rearrange("p e t -> p t e"), ALU.mult))
            link(v.tensor_reduce(ovk[:, k], tmp[:], AX.X, ALU.add))
            link(v.tensor_tensor(tot[:], ovk[:, k], slot[:, E], ALU.mult))
            link(v.tensor_tensor(sk[:, k], sk[:, k], tot[:], ALU.add))
            link(v.tensor_tensor(w[:, k], w[:, k], free[:], ALU.mult))
            link(v.tensor_tensor(w[:, k], w[:, k], ovk[:, k], ALU.add))
        link(v.tensor_scalar(sk[:], sk[:], float(P - 1), None, ALU.add))
        link(v.tensor_copy(si[:], sk[:]))
        link(v.tensor_single_scalar(hi_i[:], si[:], 7, ALU.arith_shift_right))
        link(v.tensor_single_scalar(lo_i[:], si[:], P - 1, ALU.bitwise_and))
        link(v.tensor_copy(hi_f[:], hi_i[:]))
        link(v.tensor_copy(lo_f[:], lo_i[:]))
        for e in range(E):
            if e == 0:
                link(v.tensor_scalar(te[:], iota_hi[:], cumt[:, 0:1], None, ALU.is_ge))
            else:
                link(v.scalar_tensor_tensor(out=te[:], in0=iota_hi[:], scalar=cumt[:, e:e + 1], in1=te[:], op0=ALU.is_ge, op1=ALU.add))
        link(v.tensor_copy(te_i[:], te[:]))
        for n in range(2 * T):
            k, t = n // T, n % T
            if n >= RING:
                dve.wait_ge(s_place, n - RING + 1)
            v.tensor_scalar(ring_lo[:, n % RING], iota_lo[:], lo_f[:, k, t:t + 1], None, ALU.is_equal).then_inc(s_hot, 1)
            v.tensor_scalar(ring_hi[:, n % RING], iota_hi1[:], hi_f[:, k, t:t + 1], codes[:, k, t:t + 1], ALU.is_equal,
                            ALU.mult).then_inc(s_hot, 1)
        dve.wait_ge(s_place, 2 * T)
        link(v.tensor_copy(code[:], ps[:, 1, 0:SLOT_TILES]))
        link(v.tensor_scalar(pad[:], code[:], 0.0, float(CODES + 1), ALU.is_equal, ALU.mult))
        link(v.tensor_tensor(pad[:], pad[:], code[:], ALU.add))
        link(v.tensor_scalar(pad[:], pad[:], -1.0, None, ALU.add))
        link(v.tensor_copy(dst_i[:], pad[:]))
        link(v.tensor_scalar(tokf[:], code[:], -1.0, 0.0, ALU.add, ALU.max))
        link(v.tensor_copy(tok_i[:], tokf[:]))
        link(v.tensor_single_scalar(tok_i[:], tok_i[:], 1, ALU.arith_shift_right))


def experts_block(nc, ctx, io, keep):
    def sb(name, shape, dt):
        return ctx.enter_context(nc.sbuf_tensor(name, shape, dt))

    def sem(name):
        return ctx.enter_context(nc.semaphore(name))

    N = SLOT_TILES
    tok_i, dst_i, te_i, wres, b1, b2 = (keep[n] for n in ("tok_i", "dst_i", "te_i", "wres", "b1", "b2"))
    ident16 = keep["ident16"]
    s_w = keep["s_w"]
    s_held = keep["s_held"]
    rows_in = sb("rows_in", [P, 2, 1], I32)
    rows_out = sb("rows_out", [P, 2, 1], I32)
    xg = sb("xg", [P, 2, 2 * D], F16)
    xt = sb("xt", [P, 2, 2, KC, P], F16)
    act_g = sb("act_g", [P, 2, FC, P], F32)
    g_hi = sb("g_hi", [P, 2, FC, P], F16)
    g_lo = sb("g_lo", [P, 2, FC, P], F16)
    y = sb("e_y", [P, 2, D], F32)
    ps = ctx.enter_context(nc.psum_tensor("ps_e", [P, 8, 512], F32))
    ps_x = ps[:, 0, :].bitcast(F16)
    ps_y = [ps[:, 1, 0:D], ps[:, 2, 0:D]]
    (s_ri, s_ro, s_turn, s_xt, s_h, s_g, s_g_hi, s_g_lo, s_y, s_ye, s_sc0, s_sc1, s_ga0, s_ga1) = [
        sem("e_" + n) for n in "ri ro turn xt h g g_hi g_lo y ye sc0 sc1 ga0 ga1".split()]
    s_sc, s_ga = [s_sc0, s_sc1], [s_ga0, s_ga1]
    block = ctx.enter_context(nc.Block())

    def steps(eng, step):
        step(-2, 0, "G")
        step(-1, 1, "GT")
        step(0, 0, "GTH")
        step(1, 1, "GTHO")
        step(2, 0, "GTHO")
        step(3, 1, "GTHO")
        with eng.Fori(2, N // 2 - 1, 1) as b:
            step(2 * b, 0, "GTHO")
            step(2 * b + 1, 1, "GTHO")
        step(N - 2, 0, "THO")
        step(N - 1, 1, "HO")
        step(N, 0, "O")

    def since(t, n=0):
        return not (isinstance(t, int) and t < n)

    def expert(eng, t):
        return eng.value_load(te_i[0:1, bass.ds(t, 1)], min_val=0, max_val=NE - 1)

    @block.gpsimd
    def _(pool):
        def step(k, p, stages):
            if "G" in stages:
                t = k + 2
                if since(t, 2):
                    pool.wait_ge(s_ga[p], 16 * half(t))
                nc.gpsimd.tensor_copy(rows_in[:, p], tok_i[:, bass.ds(t, 1)]).then_inc(s_ri, 1)
                if since(t, 2):
                    pool.wait_ge(s_turn, t - 1)
                pool.wait_ge(s_ri, t + 1)
                pool.sem_inc(s_held, 1)
                nc.gpsimd.indirect_dma_start(xg[:, p], None, io["pair_scr"], bass.IndirectOffsetOnAxis(ap=rows_in[:, p].bitcast(U32), axis=0)).then_inc(s_ga[p], 16)
            if "O" in stages:
                t, q = k - 1, 1 - p
                if since(t, 2):
                    pool.wait_ge(s_sc[q], 16 * half(t))
                nc.gpsimd.tensor_copy(rows_out[:, q], dst_i[:, bass.ds(t, 1)]).then_inc(s_ro, 1)
                pool.wait_ge(s_ye, t + 1)
                pool.wait_ge(s_ro, t + 1)
                pool.sem_inc(s_held, 1)
                nc.gpsimd.indirect_dma_start(io["z_scr"], bass.IndirectOffsetOnAxis(ap=rows_out[:, q].bitcast(U32), axis=0), y[:, q], None,
                                             bounds_check=CODES - 1, oob_is_err=False).then_inc(s_sc[q], 16)

        steps(pool, step)
        for q in range(2):
            pool.wait_ge(s_sc[q], 16 * N // 2)

    @block.tensor
    def _(pe):
        mm = nc.tensor.matmul

        def turn(t, p):
            if since(t, 1):
                pe.wait_ge(s_xt, t)
            pe.wait_ge(s_ga[p], 16 * (half(t) + 1))
            for n in range(2 * KC):
                last = nc.tensor.transpose(ps_x[:, n * P:(n + 1) * P], xg[:, p, n * P:(n + 1) * P], ident16[:])
            last.then_inc(s_turn, 1)

        def hidden(t, p, e):
            pe.wait_ge(s_xt, t + 1)
            if since(t, 2):
                pe.wait_ge(s_g, FC * (t - 1))
            pe.sem_inc(keep["s_held_pe"], 1)
            for f in range(FC):
                out = ps[:, 3 + 2 * p + f // 4, (f % 4) * P:(f % 4 + 1) * P]
                todo = [(a, b, c) for c in range(KC) for a, b in ((0, 0), (1, 0), (0, 1))]
                for m, (a, b, c) in enumerate(todo):
                    last = mm(out, wres[:, b, bass.ds(e * WSIZE + c * FF + f * P, P)], xt[:, p, a, c], start=(m == 0), stop=(m == 5))
                last.then_inc(s_h, 1)

        def output(t, p, e):
            pe.wait_ge(s_g_lo, t + 1)
            if since(t, 2):
                pe.wait_ge(s_ye, t - 1)
            pe.sem_inc(keep["s_held_pe"], 1)
            for f in range(FC):
                for a, b in ((g_hi, 0), (g_hi, 1), (g_lo, 0)):
                    last = mm(ps_y[p], a[:, p, f], wres[:, b, bass.ds(e * WSIZE + KC * FF + f * D, D)],
                              start=(f == 0 and a is g_hi and b == 0), stop=(f == FC - 1 and a is g_lo))
            last.then_inc(s_y, 1)

        def step(k, p, stages):
            if "T" in stages:
                turn(k + 1, 1 - p)
            if "H" in stages:
                hidden(k, p, expert(pe, k))
            if "O" in stages:
                output(k - 1, 1 - p, expert(pe, k - 1))

        for e in range(NE):
            pe.wait_ge(s_w[e], 32)
        steps(pe, step)

    @block.scalar
    def _(act):
        def step(k, p, stages):
            if "H" in stages:
                e = expert(act, k)
                if since(k, 2):
                    act.wait_ge(s_g_lo, k - 1)
                for f in range(FC):
                    act.wait_ge(s_h, FC * k + (f // 4 + 1) * 4)
                    act.sem_inc(keep["s_held_act"], 1)
                    nc.scalar.activation(act_g[:, p, f], ps[:, 3 + 2 * p + f // 4, (f % 4) * P:(f % 4 + 1) * P], ACT.Gelu,
                                         bias=b1[:, bass.ds(e * FC + f, 1)], scale=1.0 / H_UP).then_inc(s_g, 1)

        act.wait_ge(keep["s_b"], 32)
        steps(act, step)

    @block.vector
    def _(dve):
        def step(k, p, stages):
            if "T" in stages:
                t, q = k + 1, 1 - p
                dve.wait_ge(s_turn, t + 1)
                if since(t, 2):
                    dve.wait_ge(s_h, FC * (t - 1))
                nc.vector.tensor_copy(xt[:, q].rearrange("p k c n -> p (k c n)"), ps_x[:, 0:4 * P]).then_inc(s_xt, 1)
            if "O" in stages:
                t, q = k - 1, 1 - p
                e = expert(dve, t)
                dve.wait_ge(s_y, t + 1)
                if since(t, 2):
                    dve.wait_ge(s_sc[q], 16 * half(t))
                dve.sem_inc(keep["s_held_dve"], 1)
                nc.vector.scalar_tensor_tensor(out=y[:, q], in0=ps_y[q], scalar=1.0 / (G_UP * WP_UP), in1=b2[:, bass.ds(e * D, D)],
                                               op0=ALU.mult, op1=ALU.add).then_inc(s_ye, 1)
            if "H" in stages:
                dve.wait_ge(s_g, FC * (k + 1))
                if since(k, 2):
                    dve.wait_ge(s_y, k - 1)
                nc.vector.tensor_scalar(g_hi[:, p], act_g[:, p], G_UP, None, ALU.mult).then_inc(s_g_hi, 1)
                dve.wait_ge(s_g_hi, k + 1)
                nc.vector.scalar_tensor_tensor(out=g_lo[:, p], in0=act_g[:, p], scalar=G_UP, in1=g_hi[:, p], op0=ALU.mult,
                                               op1=ALU.subtract).then_inc(s_g_lo, 1)

        dve.wait_ge(keep["s_b"], 32)
        steps(dve, step)


def final_block(nc, ctx, io, keep):
    def sb(name, shape, dt):
        return ctx.enter_context(nc.sbuf_tensor(name, shape, dt))

    def sem(name):
        return ctx.enter_context(nc.semaphore(name))

    Q = 4
    N = TILES // Q
    w = keep["weights"]
    z = sb("f_z", [P, 2, Q, 2, D], F32)
    x2 = sb("f_x2", [P, 2, Q, D], F32)
    a = sb("f_a", [P, 2, Q, D], F32)
    s2 = sb("f_s2", [P, 2, Q, D], F32)
    out = sb("f_out", [P, 2, Q, D], F32)
    stats = sb("f_stats", [P, Q, 6], F32)
    mv = sb("f_mv", [P, 2, Q, 2], F32)
    ve = sb("f_ve", [P, 2, Q], F32)
    rstd = sb("f_rstd", [P, 2, Q], F32)
    nmr = sb("f_nmr", [P, 2, Q], F32)
    half4 = sb("f_half", [P, Q], F32)
    s_z = [sem("f_z0"), sem("f_z1")]
    s_out = [sem("f_o0"), sem("f_o1")]
    s_a, s_s, s_ch, s_ve, s_rstd, s_nmr, s_n, s_half = (sem("f_" + n) for n in "a s ch ve rstd nmr n half".split())
    block = ctx.enter_context(nc.Block())

    @block.sync
    def _(sp):
        for n in range(N):
            p = n % 2
            if n >= 2:
                sp.wait_ge(s_s, (n - 1) * Q)
            sp.dma_start(z[:, p], io["z_scr"].rearrange("(t p k) d -> p t k d", p=P, k=2)[:, n * Q:(n + 1) * Q]).then_inc(s_z[p], 16)
            sp.dma_start(x2[:, p], io["x2_scr"].rearrange("(t p) d -> p t d", p=P)[:, n * Q:(n + 1) * Q]).then_inc(s_z[p], 16)

    @block.scalar
    def _(act):
        def finish(n):
            p = n % 2
            act.wait_ge(s_nmr, n + 1)
            if n >= 2:
                act.wait_ge(s_out[p], 16 * (n // 2))
            for j in range(Q):
                nc.scalar.activation(out[:, p, j], s2[:, p, j], ACT.Identity, bias=nmr[:, p, j:j + 1], scale=rstd[:, p, j:j + 1]).then_inc(s_n, 1)
            act.wait_ge(s_n, (n + 1) * Q)
            act.dma_start(io["out"].rearrange("(t p) d -> p t d", p=P)[:, n * Q:(n + 1) * Q], out[:, p]).then_inc(s_out[p], 16)

        for n in range(N):
            p = n % 2
            act.wait_ge(s_z[p], 32 * (n // 2 + 1))
            if n >= 2:
                act.wait_ge(s_s, (n - 1) * Q)
            for j in range(Q):
                nc.scalar.activation(a[:, p, j], z[:, p, j, 0], ACT.Copy, scale=w[:, 0, n * Q + j:n * Q + j + 1]).then_inc(s_a, 1)
            if n >= 1:
                finish(n - 1)
        finish(N - 1)
        for p in range(2):
            act.wait_ge(s_out[p], 16 * (N // 2))

    @block.gpsimd
    def _(pool):
        nc.gpsimd.memset(half4[:], -0.5).then_inc(s_half, 1)
        pool.wait_ge(s_half, 1)
        for n in range(N):
            p = n % 2
            pool.wait_ge(s_ve, n + 1)
            nc.gpsimd.tensor_tensor(rstd[:, p], ve[:, p], half4[:], ALU.pow).then_inc(s_rstd, 1)

    @block.vector
    def _(dve):
        done = [0]

        def link(ins):
            done[0] += 1
            ins.then_inc(s_ch, 1)
            dve.wait_ge(s_ch, done[0])

        for n in range(N):
            p = n % 2
            if n >= 2:
                dve.wait_ge(s_n, (n - 1) * Q)
            for j in range(Q):
                dve.wait_ge(s_a, n * Q + j + 1)
                link(nc.vector.scalar_tensor_tensor(out=s2[:, p, j], in0=z[:, p, j, 1], scalar=w[:, 1, n * Q + j:n * Q + j + 1],
                                                    in1=a[:, p, j], op0=ALU.mult, op1=ALU.add))
                nc.vector.tensor_tensor(s2[:, p, j], s2[:, p, j], x2[:, p, j], ALU.add).then_inc(s_s, 1)
                dve.wait_ge(s_s, n * Q + j + 1)
                link(nc.vector.bn_stats(stats[:, j], s2[:, p, j]))
                link(nc.vector.bn_aggr(mv[:, p, j], stats[:, j]))
            nc.vector.tensor_scalar(ve[:, p], mv[:, p, :, 1], EPS, None, ALU.add).then_inc(s_ve, 1)
            dve.wait_ge(s_rstd, n + 1)
            nc.vector.scalar_tensor_tensor(out=nmr[:, p], in0=mv[:, p, :, 0], scalar=-1.0, in1=rstd[:, p], op0=ALU.mult,
                                           op1=ALU.mult).then_inc(s_nmr, 1)


def program(nc, io):
    with ExitStack() as ctx:
        def sb(name, shape, dt):
            return ctx.enter_context(nc.sbuf_tensor(name, shape, dt))

        keep = {
            "ident": sb("ident", [P, P], F32),
            "ident16": sb("ident16", [P, P], F16),
            "neg_half": sb("neg_half", [P, 1], F32),
            "logits": sb("logits", [P, TILES * E], F32),
            "weights": sb("weights", [P, 2, TILES], F32),
            "tok_i": sb("tok_i", [P, SLOT_TILES], I32),
            "dst_i": sb("dst_i", [P, SLOT_TILES], I32),
            "te_i": sb("te_i", [P, SLOT_TILES], I32),
        }
        for n in ("s_held", "s_held_pe", "s_held_act", "s_held_dve", "s_held_pool", "s_held_sp", "s_b"):
            keep[n] = ctx.enter_context(nc.semaphore(n))
        keep["s_w"] = [ctx.enter_context(nc.semaphore("s_w%d" % e)) for e in range(NE)]
        with ExitStack() as phase:
            attention_block(nc, phase, io, keep)
        with ExitStack() as phase:
            keep["wres"] = phase.enter_context(nc.sbuf_tensor("wres", [P, 2, NE * WSIZE], F16))
            keep["b1"] = phase.enter_context(nc.sbuf_tensor("b1", [P, NE * FC], F32))
            keep["b2"] = phase.enter_context(nc.sbuf_tensor("b2", [P, NE * D], F32))
            with ExitStack() as part:
                routing_block(nc, part, io, keep)
            with ExitStack() as part:
                experts_block(nc, part, io, keep)
        with ExitStack() as phase:
            final_block(nc, phase, io, keep)


def kernel(**inputs):
    import numpy as _np
    import concourse.bacc as _bacc
    from concourse import mybir as _mybir
    from concourse.bass_utils import run_bass_kernel_spmd as _run

    nc = _bacc.Bacc("TRN2", target_bir_lowering=False, num_devices=1)
    a = {k: _np.asarray(v) for k, v in inputs.items()}
    up = _np.concatenate([a["L0_ffn_W1"], a["L0_ffn_fw1"][None]])
    down = _np.concatenate([a["L0_ffn_W2"], a["L0_ffn_fw2"][None]])
    moe_w = _np.concatenate([up.reshape(NE, KC, P, FF).transpose(2, 0, 1, 3).reshape(P, NE, -1),
                             down.reshape(NE, FC, P, D).transpose(2, 0, 1, 3).reshape(P, NE, -1)], axis=2)
    lay = {
        "x": a["x"].reshape(TOKENS, D),
        "xT": a["x"].reshape(TOKENS, D).T,
        "ctxT": a["ctx_1024"].transpose(2, 0, 1).reshape(D, BATCH * CTX),
        "mask": a["mask_1x1xSxS2_ik0"].reshape(SEQ, CTX),
        "wq": a["L0_attn_Wq"].transpose(1, 0, 2).reshape(D, H * HS),
        "wk": a["L0_attn_Wk"].transpose(1, 0, 2).reshape(D, H * HS),
        "wv": a["L0_attn_Wv"].transpose(1, 0, 2).reshape(D, H * HS),
        "proj": a["L0_attn_proj_w"].T,
        "proj_b": a["L0_attn_proj_b"],
        "xwq": a["L0_xattn_w_q"].T, "xwk": a["L0_xattn_w_k"].T, "xwv": a["L0_xattn_w_v"].T, "xwo": a["L0_xattn_w_o"].T,
        "wr": a["L0_ffn_Wr"].T,
        "moe_w": moe_w.reshape(P, NE * WSIZE),
        "b1T": _np.concatenate([a["L0_ffn_b1"], a["L0_ffn_fb1"][None]]).reshape(NE, FC, P).transpose(2, 0, 1).reshape(P, NE * FC),
        "b2": _np.concatenate([a["L0_ffn_b2"], a["L0_ffn_fb2"][None]]).reshape(NE * D),
    }
    arrays, io = {}, {}
    for name, v in lay.items():
        v = _np.ascontiguousarray(v)
        arrays["in_" + name] = v
        io[name] = nc.dram_tensor("in_" + name, v.shape, _mybir.dt.from_np(v.dtype), kind="ExternalInput").ap()
    for name, shape, dt in (("v_scr", (2, P, 2 * H * HS), F16), ("pair_scr", (TOKENS, 2 * D), F16), ("x2_scr", (TOKENS, D), F32),
                            ("z_scr", (CODES, D), F32), ("w_scr", (2, P, NE * WSIZE), F16)):
        io[name] = nc.dram_tensor(name, shape, dt, kind="Internal").ap()
    io["out"] = nc.dram_tensor("out_0", (TOKENS, D), F32, kind="ExternalOutput").ap()
    program(nc, io)
    r = _run(nc, [arrays], core_ids=[0])
    return r.results[0]["out_0"].reshape(BATCH, SEQ, D)
```

```python
from contextlib import ExitStack

import concourse.bass as bass
from concourse import mybir

F32 = mybir.dt.float32
F16 = mybir.dt.float16
I32 = mybir.dt.int32
U32 = mybir.dt.uint32
ALU = mybir.AluOpType
ACT = mybir.ActivationFunctionType
AX = mybir.AxisListType

P = 128
BATCH, SEQ, D = 16, 256, 256
TOKENS = BATCH * SEQ
TILES = TOKENS // P
H, HS = 16, 64
GTOK = SEQ // H
GROUPS = P // GTOK
KC = D // P
CTX, DK = 77, 16
HB = P // DK
E = 8
NE = E + 1
FF = 1024
WSIZE = 2 * D * FF // P
PIECES = TILES - 8
PIECE = NE * WSIZE // PIECES
FC = FF // P
CAP = int(1.25 * (TOKENS * 2 / E))
EPS = 1e-5

X_UP = 4.0
WA_UP = 16.0
WP_UP = 64.0
QK_UP = X_UP * WA_UP
SCORE_SCALE = HS ** -0.5 / QK_UP ** 2
SCORE2_SCALE = DK ** -0.5 / QK_UP ** 2
NEG2 = -1e9 / SCORE2_SCALE

FILLS = [("v", 0), ("q", 0), ("v", 1), ("q", 1), ("q", 2), ("q", 3), ("k", 0), ("k", 1), ("k", 2), ("k", 3)]
NF = len(FILLS)
V_FILLS = 3
FILLS_OF_SLOT = [[2, 3], [], [4], [5], [6, 7], [8], [9], []]


EARLY = (4, 0, 1, 1, 0, 1, 1, 2)


def fills_of(s, p, g, stages):
    if g == GROUPS - 1:
        return [(s + 2, p, 0), (s + 2, p, 1)] if "N" in stages else []
    first = [(0, 0, 0), (0, 0, 1)] if g == 0 and isinstance(s, int) and s == -1 else []
    return first + ([(s + 1, 1 - p, j) for j in FILLS_OF_SLOT[g]] if "A" in stages else [])


def attention_block(nc, ctx, io, keep):
    def sb(name, shape, dt):
        return ctx.enter_context(nc.sbuf_tensor(name, shape, dt))

    def sem(name):
        return ctx.enter_context(nc.semaphore(name))

    wqk = {n: sb("w2_" + n, [P, 2, KC, H, 2, HS], F16) for n in "qk"}
    wv = sb("wv_pair", [P, 2, KC, H * HS], F16)
    wp = sb("proj_pair", [P, 2, H, D], F16)
    w2 = {n: sb("xw_" + n, [P, 2, KC, D], F16) for n in ("q", "k", "v", "o")}
    wr = sb("wr", [P, KC, E], F32)
    proj_b = sb("proj_b", [P, D], F32)
    ident = keep["ident"]
    ident16 = keep["ident16"]
    ident_big = sb("ident_big", [P, P], F16)
    causal = sb("causal", [P, P], F16)
    lo_rows = sb("lo_rows", [P, 1], F32)
    head_rows = sb("head_rows", [P, HB, CTX], F16)
    mask = sb("mask", [P, 2, CTX], I32)
    neg_half = keep["neg_half"]
    eps = sb("eps", [P, 1], F32)
    zero = sb("zero", [P, 2 * D], F32)
    s_held_dve, s_held_pool, s_held_sp = keep["s_held_dve"], keep["s_held_pool"], keep["s_held_sp"]

    with ExitStack() as tmp:
        stage = {n: tmp.enter_context(nc.sbuf_tensor("st_" + n, [P, KC, D * 4], F32)) for n in "qkv"}
        stage_p = tmp.enter_context(nc.sbuf_tensor("st_p", [P, H, D], F32))
        stage_x = {n: tmp.enter_context(nc.sbuf_tensor("st_x" + n, [P, KC, D], F32)) for n in ("q", "k", "v", "o")}
        ld = {n: tmp.enter_context(nc.semaphore("ld_" + n)) for n in ("q", "k", "v", "p", "xq", "xk", "xv", "xo")}
        s_small = tmp.enter_context(nc.semaphore("s_small"))
        s_hi = tmp.enter_context(nc.semaphore("s_hi"))
        s_lo = tmp.enter_context(nc.semaphore("s_lo"))
        s_const = tmp.enter_context(nc.semaphore("s_const"))
        block = tmp.enter_context(nc.Block())

        @block.sync
        def _(sp):
            for n in "qkv":
                sp.dma_start(stage[n][:], io["w" + n].rearrange("(c p) n -> p c n", p=P)).then_inc(ld[n], 16)
            for half in range(2):
                sp.dma_start(stage_p[half * HS:(half + 1) * HS], io["proj"].rearrange("(h d) n -> d h n", d=HS)).then_inc(ld["p"], 16)
            for n in ("q", "k", "v", "o"):
                sp.dma_start(stage_x[n][:], io["xw" + n].rearrange("(c p) n -> p c n", p=P)).then_inc(ld["x" + n], 16)
            sp.dma_start(wr[:], io["wr"].rearrange("(c p) n -> p c n", p=P)).then_inc(s_small, 16)
            sp.dma_start(proj_b[:], io["proj_b"].rearrange("(a n) -> a n", a=1).partition_broadcast(P)[:, 0, :]).then_inc(s_small, 16)
            sp.dma_start(mask[:], io["mask"].rearrange("(c p) k -> p c k", p=P)).then_inc(s_small, 16)
            sp.wait_ge(s_small, 48)

        pairs = []
        for n in "qk":
            for copy in range(2):
                pairs.append((ld[n], 16, stage[n][:].rearrange("p c (h d) -> p c h d", d=HS),
                              [wqk[n][:, k, :, :, copy, :] for k in range(2)], WA_UP))
        pairs.append((ld["v"], 16, stage["v"][:], [wv[:, k] for k in range(2)], WA_UP))
        pairs.append((ld["p"], 32, stage_p[:], [wp[:, k] for k in range(2)], WP_UP))
        for n in ("q", "k", "v", "o"):
            pairs.append((ld["x" + n], 16, stage_x[n][:], [w2[n][:, k] for k in range(2)], WA_UP))

        @block.scalar
        def _(act):
            for s, v, src, (hi, lo), up in pairs:
                act.wait_ge(s, v)
                for c in range(src.shape[1]):
                    last = nc.scalar.activation(hi[:, c], src[:, c], ACT.Copy, scale=up)
                last.then_inc(s_hi, 1)

        @block.vector
        def _(dve):
            for n, (s, v, src, (hi, lo), up) in enumerate(pairs):
                dve.wait_ge(s, v)
                dve.wait_ge(s_hi, n + 1)
                for c in range(src.shape[1]):
                    nc.vector.scalar_tensor_tensor(out=lo[:, c], in0=src[:, c], scalar=up, in1=hi[:, c],
                                                   op0=ALU.mult, op1=ALU.subtract).then_inc(s_lo, 1)

        @block.gpsimd
        def _(pool):
            n = 0
            for ins in (nc.gpsimd.memset(ident[:], 0.0), nc.gpsimd.memset(ident16[:], 0.0), nc.gpsimd.memset(ident_big[:], 0.0),
                        nc.gpsimd.memset(causal[:], 0.0), nc.gpsimd.memset(lo_rows[:], 0.0), nc.gpsimd.memset(head_rows[:], 1.0),
                        nc.gpsimd.memset(neg_half[:], -0.5), nc.gpsimd.memset(eps[:], EPS),
                        nc.gpsimd.memset(zero[:], 0.0)):
                ins.then_inc(s_const, 1)
                n += 1
            pool.wait_ge(s_const, n)
            for m, one in ((ident, 1.0), (ident16, 1.0), (ident_big, 32768.0)):
                nc.gpsimd.affine_select(out=m[:], in_=m[:], compare_op=ALU.not_equal, fill=one, base=0,
                                        pattern=[[-1, P]], channel_multiplier=1).then_inc(s_const, 1)
            nc.gpsimd.affine_select(out=causal[:], in_=causal[:], compare_op=ALU.is_ge, fill=-65504.0, base=0,
                                    pattern=[[-1, P]], channel_multiplier=1).then_inc(s_const, 1)
            nc.gpsimd.affine_select(out=lo_rows[:], in_=lo_rows[:], compare_op=ALU.is_gt, fill=-1.0, base=HS,
                                    pattern=[[0, 1]], channel_multiplier=-1).then_inc(s_const, 1)
            nc.gpsimd.affine_select(out=head_rows[:], in_=head_rows[:], compare_op=ALU.is_ge, fill=0.0, base=0,
                                    pattern=[[-DK, HB], [0, CTX]], channel_multiplier=1).then_inc(s_const, 1)
            pool.wait_ge(s_const, n + 6)
            nc.gpsimd.affine_select(out=head_rows[:], in_=head_rows[:], compare_op=ALU.is_ge, fill=0.0, base=DK - 1,
                                    pattern=[[DK, HB], [0, CTX]], channel_multiplier=-1).then_inc(s_const, 1)

    x_t = sb("x_t", [P, 2, KC, P], F32)
    x_up = sb("x_up", [P, KC, P], F32)
    ctx_up = sb("ctx_up", [P, KC, CTX], F32)
    x2_up = sb("x2_up", [P, D], F32)
    x_nat = sb("x_nat", [P, 2, D], F32)
    x_hi = sb("x_hi", [P, 2, KC, P], F16)
    x_lo = sb("x_lo", [P, 2, KC, P], F16)
    q_hi = sb("q_hi", [P, 2, 4, P], F16)
    q_st = sb("q_st", [P, 2, P, H], F16)
    k_hi = sb("k_hi", [P, 2, P, H], F16)
    k_lo = sb("k_lo", [P, 2, P, H], F16)
    v_tok = sb("v_tok", [P, 2, H, 2, HS], F16)
    v_pos = sb("v_pos", [P, 2, 2 * GROUPS, 2, HS], F16)
    nmax = sb("nmax", [P, 2], F32)
    nbias = sb("nbias", [P, 2], F32)
    probs = sb("probs", [P, 384], F32)
    den = sb("den", [P, 2, 4], F32)
    rden = sb("rden", [P, 4], F32)
    pt_hi = sb("pt_hi", [P, 384], F16)
    pt_lo = sb("pt_lo", [P, 384], F16)
    o_norm = sb("o_norm", [P, 4, HS], F32)
    o_st = sb("o_st", [P, 2, 2 * GROUPS, 2, HS], F16)
    o_t = sb("o_t", [P, P, H], F16)
    x_bias = sb("x_bias", [P, D], F32)
    y1 = sb("y1", [P, D], F32)
    y2 = sb("y2", [P, D], F32)
    stats = sb("stats", [P, 2, 6], F32)
    mv = sb("mv", [P, 2, 2], F32)
    var_eps = sb("var_eps", [P, 2], F32)
    rstd = sb("rstd", [P, 2], F32)
    x1 = sb("x1", [P, 2, D], F32)
    x1_hi = sb("x1_hi", [P, KC, P], F16)
    x1_lo = sb("x1_lo", [P, KC, P], F16)
    ctx_t = sb("ctx_t", [P, KC, CTX], F32)
    c_hi = sb("c_hi", [P, KC, CTX], F16)
    c_lo = sb("c_lo", [P, KC, CTX], F16)
    q2_hi = sb("q2_hi", [P, KC, P], F16)
    q2_lo = sb("q2_lo", [P, KC, P], F16)
    k2 = sb("k2", [P, 2, KC, CTX], F16)
    k2_bd = sb("k2_bd", [P, 2, KC, HB, CTX], F16)
    v2 = sb("v2", [CTX, 2, D], F16)
    sm = sb("sm", [P, 2, HB, CTX], F32)
    mx2 = sb("mx2", [P, HB], F32)
    sm_shift = sb("sm_shift", [P, HB, CTX], F32)
    probs2 = sb("probs2", [P, HB, CTX], F32)
    den2 = sb("den2", [P, 2, H], F32)
    rden2 = sb("rden2", [P, H], F32)
    pt2_hi = sb("pt2_hi", [CTX, HB, P], F16)
    pt2_lo = sb("pt2_lo", [CTX, HB, P], F16)
    o2_norm = sb("o2_norm", [P, H, DK], F32)
    o2_hi = sb("o2_hi", [P, KC, P], F16)
    o2_lo = sb("o2_lo", [P, KC, P], F16)
    x2 = sb("x2", [P, 2, D], F32)
    x2_pair = sb("x2_pair", [P, 2, 2, D], F16)
    x2_t = sb("x2_t", [P, KC, P], F32)
    logits = keep["logits"]
    piece = sb("piece", [P, PIECE], F32)
    piece_pair = sb("piece_pair", [P, 2, PIECE], F16)

    ps = ctx.enter_context(nc.psum_tensor("ps", [P, 8, 512], F32))
    ps_a = [ps[:, 0, :], ps[:, 1, :]]
    ps_s, ps_t, ps_o = ps[:, 2, :], ps[:, 3, :], ps[:, 4, :]
    c5, c6, c7 = ps[:, 5, :], ps[:, 6, :], ps[:, 7, :]

    (s_xt, s_xn, s_ctx, s_x_hi, s_x_lo, s_fill, s_fill_hi, s_fill_lo, s_v_out, s_v_in, s_scores, s_max, s_nbias,
     s_exp, s_pt, s_pt_hi, s_pt_lo, s_pv, s_rden, s_o_norm, s_o_hi, s_o_lo, s_ot, s_ot_a, s_ot_d, s_proj, s_y1,
     s_ln1, s_var1, s_rstd1, s_x1, s_x1t, s_x1_hi, s_x1_lo, s_c_hi, s_c_lo, s_q2, s_q2_hi, s_q2_lo, s_kv2, s_kv2_hi,
     s_kv2_lo, s_bd, s_s2, s_pred, s_mx2, s_shift, s_exp2, s_den2, s_t2, s_t2_hi, s_t2_lo, s_pv2, s_rden2, s_o2n,
     s_o2t, s_o2_hi, s_o2_lo, s_proj2, s_y2, s_ln2, s_var2, s_rstd2, s_x2, s_x2_hi, s_x2_lo, s_x2t, s_x2tc, s_lg,
     s_lgc, s_out_x2, s_out_pair, s_neg) = [sem("s1_%d_%s" % (n, m)) for n, m in enumerate(
        "xt xn ctx x_hi x_lo fill fill_hi fill_lo v_out v_in scores max nbias exp pt pt_hi pt_lo pv rden o_norm o_hi "
        "o_lo ot ot_a ot_d proj y1 ln1 var1 rstd1 x1 x1t x1_hi x1_lo c_hi c_lo q2 q2_hi q2_lo kv2 kv2_hi kv2_lo bd s2 "
        "pred mx2 shift exp2 den2 t2 t2_hi t2_lo pv2 rden2 o2n o2t o2_hi o2_lo proj2 y2 ln2 var2 rstd2 x2 x2_hi x2_lo "
        "x2t x2tc lg lgc out_x2 out_pair neg".split())]

    s_z_out = sem("s1_z_out")
    s_xb, s_mv1, s_mv2 = sem("s1_xb"), sem("s1_mv1"), sem("s1_mv2")
    s_w_in, s_w_hi, s_w_lo, s_w_out = (sem("s1_" + n) for n in ("w_in", "w_hi", "w_lo", "w_out"))
    s_xt, s_xn, s_out_x2, s_out_pair = ([s, sem("s1_odd_%d" % n)] for n, s in enumerate((s_xt, s_xn, s_out_x2, s_out_pair)))

    block = ctx.enter_context(nc.Block())

    def steps(eng, step):
        step(-1, 1, "NA")
        step(0, 0, "NAB")
        step(1, 1, "NABC")
        step(2, 0, "NABCD")
        step(3, 1, "NABCD")
        with eng.Fori(2, BATCH - 2, 1) as b:
            step(2 * b, 0, "NABCDW")
            step(2 * b + 1, 1, "NABCDW")
        step(TILES - 4, 0, "NABCD")
        step(TILES - 3, 1, "NABCD")
        step(TILES - 2, 0, "ABCD")
        step(TILES - 1, 1, "BCD")
        step(TILES, 0, "CD")
        step(TILES + 1, 1, "D")

    def since(t, n=0):
        return not (isinstance(t, int) and t < n)

    @block.sync
    def _(sp):
        def load_x(t, p):
            if since(t, 2):
                sp.wait_ge(s_x_lo, t - 1)
                sp.sem_inc(s_held_sp, 1)
            sp.dma_start(x_t[:, p], io["xT"].rearrange("(c p) n -> p c n", p=P)[:, :, bass.ds(t * P, P)]).then_inc(s_xt[p], 16)

        def step(s, p, stages):
            q = 1 - p
            if "W" in stages:
                n = s - 4
                sp.wait_ge(s_w_lo, 3 * n + 1)
                sp.sem_inc(s_held_sp, 1)
                sp.dma_start(piece[:], io["moe_w"][:, bass.ds(n * PIECE, PIECE)]).then_inc(s_w_in, 16)
            if isinstance(s, int) and s == -1:
                load_x(0, 0)
                load_x(1, 1)
            elif not (isinstance(s, int) and s + 2 >= TILES):
                load_x(s + 2, p)
            if "A" in stages:
                t = s + 1
                sp.wait_ge(s_fill_hi, NF * t + V_FILLS)
                sp.sem_inc(s_held_sp, 1)
                sp.wait_ge(s_fill_lo, NF * t + V_FILLS)
                sp.sem_inc(s_held_sp, 1)
                if since(t, 2):
                    sp.wait_ge(s_v_in, 16 * (t - 1))
                    sp.sem_inc(s_held_sp, 1)
                sp.dma_start(io["v_scr"][q], v_tok[:, q].rearrange("p h k d -> p (h k d)")).then_inc(s_v_out, 16)
                sp.wait_ge(s_v_out, 16 * (t + 1))
                sp.sem_inc(s_held_sp, 1)
                if since(t, 2):
                    sp.wait_ge(s_pv, GROUPS * (t - 1))
                    sp.sem_inc(s_held_sp, 1)
                sp.dma_start(v_pos[:, q].rearrange("p g k d -> p g (k d)"),
                             io["v_scr"][q].rearrange("(g t) (h e) -> (t h) g e", t=GTOK // 2, h=H)).then_inc(s_v_in, 16)
            if "B" in stages:
                t = s
                if since(t, 2):
                    sp.wait_ge(s_xb, t - 1)
                    sp.sem_inc(s_held_sp, 1)
                sp.dma_start(x_nat[:, p], io["x"][bass.ds(t * P, P), :]).then_inc(s_xn[p], 16)
                if p == 0:
                    if since(t, 2):
                        sp.wait_ge(s_c_lo, half(t))
                        sp.sem_inc(s_held_sp, 1)
                    sp.dma_start(ctx_t[:], io["ctxT"].rearrange("(c p) n -> p c n", p=P)[:, :, bass.ds(half(t) * CTX, CTX)]
                                 ).then_inc(s_ctx, 16)
            if isinstance(s, int) and 0 <= s < 4:
                z = io["z_scr"].rearrange("(p n) d -> p (n d)", p=P)
                for n in range(s * z.shape[1] // 4, (s + 1) * z.shape[1] // 4, 2 * D):
                    sp.dma_start(z[:, n:n + 2 * D], zero[:]).then_inc(s_z_out, 16)
            if "D" in stages:
                t = s - 2
                sp.wait_ge(s_x2, t + 1)
                sp.sem_inc(s_held_sp, 1)
                sp.dma_start(io["x2_scr"][bass.ds(t * P, P), :], x2[:, p]).then_inc(s_out_x2[p], 16)
                sp.wait_ge(s_x2_lo, t + 1)
                sp.sem_inc(s_held_sp, 1)
                sp.dma_start(io["pair_scr"][bass.ds(t * P, P), :], x2_pair[:, p].rearrange("p k d -> p (k d)")).then_inc(s_out_pair[p], 16)

            if "W" in stages:
                sp.wait_ge(s_w_lo, 3 * n + 4)
                sp.sem_inc(s_held_sp, 1)
                sp.dma_start(io["w_scr"].rearrange("k p n -> p k n")[:, :, bass.ds(n * PIECE, PIECE)], piece_pair[:]).then_inc(s_w_out, 16)

        steps(sp, step)
        sp.wait_ge(s_z_out, 16 * (CODES // P) // 2)
        sp.wait_ge(s_w_out, 16 * (PIECES + 1))
        for p in range(2):
            sp.wait_ge(s_out_x2[p], 16 * BATCH)
            sp.wait_ge(s_out_pair[p], 16 * BATCH)

    @block.tensor
    def _(pe):
        mm = nc.tensor.matmul

        def fill(t, p, j):
            kind, n = FILLS[j]
            if j == 0:
                pe.wait_ge(s_x_lo, t + 1)
            if since(t, 1) or j >= 2:
                pe.wait_ge(s_fill_lo, NF * t + j - 1)
            bank = ps_a[j % 2]
            xs = (x_hi[:, p], x_lo[:, p])
            if kind == "v":
                steps_ = [(a, b, c) for c in range(KC) for a, b in ((0, 0), (0, 1), (1, 0))]
                for m, (a, b, c) in enumerate(steps_):
                    last = mm(bank, xs[a][:, c], wv[:, b, c, n * 512:(n + 1) * 512], start=(m == 0), stop=(m == 5))
            else:
                for hh in range(4):
                    h = 4 * n + hh
                    w = wqk[kind]
                    steps_ = [(a, b, c) for c in range(KC) for a, b in ((0, 0), (1, 0), (0, 1))]
                    for m, (a, b, c) in enumerate(steps_):
                        last = mm(bank[:, hh * P:(hh + 1) * P], w[:, b, c, h].rearrange("p k d -> p (k d)"), xs[a][:, c],
                                  start=(m == 0), stop=(m == 5))
            last.then_inc(s_fill, 1)

        def scores(t, p, g):
            if g == 0:
                pe.wait_ge(s_fill_lo, NF * (t + 1))
            if since(t, 1) or g:
                pe.wait_ge(s_exp, 2 * (GROUPS * t + g))
            qs, kh, kl = (m[:, p, g * GTOK:(g + 1) * GTOK].rearrange("p t h -> p (t h)") for m in (q_st, k_hi, k_lo))
            mm(ps_s[:, 0:P], qs[:, 0:P], kh[:, 0:P], start=True, stop=False, skip_group_check=True)
            mm(ps_s[:, 0:P], qs[:, 0:P], kl[:, 0:P], start=False, stop=False, skip_group_check=True)
            mm(ps_s[:, 0:P], ident_big[:], causal[:], start=False, stop=True, skip_group_check=True)
            mm(ps_s[:, P:384], qs[:, P:256], kh[:, :], start=False, stop=False, skip_group_check=True)
            mm(ps_s[:, P:384], qs[:, P:256], kl[:, :], start=False, stop=False, skip_group_check=True)
            mm(ps_s[:, 256:384], ident_big[:], causal[:], start=False, stop=True,
               skip_group_check=True).then_inc(s_scores, 1)

        def turn_probs(t, g):
            pe.wait_ge(s_exp, 2 * (GROUPS * t + g) + 2)
            if since(t, 1) or g:
                pe.wait_ge(s_pt_lo, GROUPS * t + g)
            for b in range(3):
                last = nc.tensor.transpose(ps_t[:, b * P:(b + 1) * P], probs[:, b * P:(b + 1) * P], ident[:])
            last.then_inc(s_pt, 1)

        def pv(t, p, g):
            pe.wait_ge(s_pt_lo, GROUPS * t + g + 1)
            if g == 0:
                pe.wait_ge(s_v_in, 16 * (t + 1))
            if g % 2 == 0 and (since(t, 1) or g):
                pe.wait_ge(s_o_norm, 4 * t + g // 2)
            for q in range(2):
                out = ps_o[:, (g % 2 * 2 + q) * HS:(g % 2 * 2 + q + 1) * HS]
                blocks = [(0, 0)] if q == 0 else [(1, 0), (2, 1)]
                todo = [(a, b, blk, c) for blk, c in blocks for a, b in ((pt_hi, 0), (pt_hi, 1), (pt_lo, 0))]
                for m, (a, b, blk, c) in enumerate(todo):
                    last = mm(out, a[:, blk * P:(blk + 1) * P], v_pos[:, p, 2 * g + c, b], start=(m == 0), stop=(m == len(todo) - 1))
            last.then_inc(s_pv, 1)

        def stage_c(t, p, g):
            if g == 0:
                pe.wait_ge(s_o_lo, 4 * (t + 1))
                if since(t, 1):
                    pe.wait_ge(s_t2_lo, 4 * t)
                for half_, bank in enumerate((c5, c6)):
                    b16 = bank.bitcast(F16)
                    for n in range(8):
                        last = nc.tensor.transpose(b16[:, n * P:(n + 1) * P], o_st[:, p, 8 * half_ + n].rearrange("p k d -> p (k d)"), ident16[:])
                    last.then_inc(s_ot, 1)
            if g == 1:
                pe.wait_ge(s_ot_a, t + 1)
                pe.wait_ge(s_ot_d, t + 1)
                if p == 0:
                    pe.wait_ge(s_c_lo, half(t) + 1)
                    for o in range(KC):
                        todo = [(a, b, c) for c in range(KC) for a, b in ((0, 0), (1, 0), (0, 1))]
                        for m, (a, b, c) in enumerate(todo):
                            mm(c6[:, o * CTX:(o + 1) * CTX], w2["k"][:, b, c, o * P:(o + 1) * P], (c_hi, c_lo)[a][:, c],
                               start=(m == 0), stop=(m == 5))
                    for m, (a, b, c) in enumerate(todo):
                        last = mm(c6[0:CTX, 256:512], (c_hi, c_lo)[a][:, c], w2["v"][:, b, c], start=(m == 0), stop=(m == 5))
                    last.then_inc(s_kv2, 1)
                for h in range(H):
                    for k in range(2):
                        last = mm(c5[:, 0:D], o_t[:, :, h], wp[:, k, h], start=(h == 0 and k == 0), stop=(h == H - 1 and k == 1))
                last.then_inc(s_proj, 1)
            if g == 2:
                pe.wait_ge(s_x1, t + 1)
                if p == 0:
                    pe.wait_ge(s_kv2_lo, 2 * (half(t) + 1))
                for c in range(KC):
                    last = nc.tensor.transpose(c6[:, c * P:(c + 1) * P], x1[:, p, c * P:(c + 1) * P], ident[:])
                last.then_inc(s_x1t, 1)
            if g == 3:
                pe.wait_ge(s_x1_lo, t + 1)
                pe.wait_ge(s_y1, t + 1)
                for o in range(KC):
                    todo = [(a, b, c) for c in range(KC) for a, b in ((0, 0), (1, 0), (0, 1))]
                    for m, (a, b, c) in enumerate(todo):
                        last = mm(c5[:, o * P:(o + 1) * P], w2["q"][:, b, c, o * P:(o + 1) * P], (x1_hi, x1_lo)[a][:, c],
                                  start=(m == 0), stop=(m == 5))
                last.then_inc(s_q2, 1)
            if g in (4, 6):
                cc = (g - 4) // 2
                if cc == 1:
                    pe.wait_ge(s_t2_lo, 4 * t + 2)
                else:
                    pe.wait_ge(s_q2_lo, t + 1)
                    pe.wait_ge(s_bd, 4 * (half(t) + 1))
                for j, bank in enumerate((c5, c6)):
                    out = bank[:, 0:4 * CTX]
                    for m, (a, b) in enumerate(((q2_hi, 0), (q2_lo, 0), (q2_hi, 1))):
                        last = mm(out, a[:, cc], k2_bd[:, b, cc, 4 * j:4 * j + 4].rearrange("p h k -> p (h k)"), start=(m == 0), stop=(m == 2))
                last.then_inc(s_s2, 1)
            if g in (5, 7):
                cc = (g - 5) // 2
                pe.wait_ge(s_exp2, 2 * t + cc + 1)
                pe.wait_ge(s_pred, 4 * t + 2 * cc + 2)
                for j, bank in enumerate((c5, c6)):
                    for n in range(4):
                        last = nc.tensor.transpose(bank[0:CTX, n * P:(n + 1) * P], probs2[:, 4 * j + n], ident[:])
                    last.then_inc(s_t2, 1)

        def pv2(t, cc):
            if cc == 0 and since(t, 1):
                pe.wait_ge(s_lgc, t)
            for n in range(HB):
                h = HB * cc + n
                for m, (a, b) in enumerate(((pt2_hi, 0), (pt2_lo, 0), (pt2_hi, 1))):
                    last = mm(c7[:, h * DK:(h + 1) * DK], a[:, n], v2[:, b, h * DK:(h + 1) * DK], start=(m == 0), stop=(m == 2))
            last.then_inc(s_pv2, 1)

        def stage_d(t, p, g):
            if g == 0:
                pe.wait_ge(s_t2_lo, 4 * t + 4)
                pv2(t, 1)
            if g == 1:
                pe.wait_ge(s_o2n, t + 1)
                o = o2_norm[:].rearrange("p h d -> p (h d)")
                for c in range(KC):
                    last = nc.tensor.transpose(c7[:, c * P:(c + 1) * P], o[:, c * P:(c + 1) * P], ident[:])
                last.then_inc(s_o2t, 1)
            if g == 2:
                pe.wait_ge(s_o2_lo, t + 1)
                todo = [(a, b, c) for c in range(KC) for a, b in ((0, 0), (1, 0), (0, 1))]
                for m, (a, b, c) in enumerate(todo):
                    last = mm(c7[:, 0:D], (o2_hi, o2_lo)[a][:, c], w2["o"][:, b, c], start=(m == 0), stop=(m == 5))
                last.then_inc(s_proj2, 1)
            if g == 3:
                pe.wait_ge(s_x2, t + 1)
                for c in range(KC):
                    last = nc.tensor.transpose(c7[:, c * P:(c + 1) * P], x2[:, p, c * P:(c + 1) * P], ident[:])
                last.then_inc(s_x2t, 1)
            if g == 4:
                pe.wait_ge(s_x2tc, t + 1)
                for c in range(KC):
                    last = mm(c7[:, 0:E], x2_t[:, c], wr[:, c], start=(c == 0), stop=(c == KC - 1))
                last.then_inc(s_lg, 1)

        def step(s, p, stages):
            for g in range(GROUPS):
                if "B" in stages:
                    turn_probs(s, g)
                fills = fills_of(s, p, g, stages)
                if g == 7 and fills:
                    fill(*fills.pop(0))
                if "B" in stages and g < GROUPS - 1:
                    scores(s, p, g + 1)
                elif "A" in stages and g == GROUPS - 1:
                    scores(s + 1, 1 - p, 0)
                for t, q, j in fills[:EARLY[g]]:
                    fill(t, q, j)
                if "D" in stages and g < 3:
                    stage_d(s - 2, p, g)
                if "C" in stages:
                    stage_c(s - 1, 1 - p, g)
                for t, q, j in fills[EARLY[g]:]:
                    fill(t, q, j)
                if "C" in stages and g == 6:
                    pv2(s - 1, 0)
                if "B" in stages:
                    pv(s, p, g)
                if "D" in stages and g >= 3:
                    stage_d(s - 2, p, g)

        steps(pe, step)

    @block.scalar
    def _(act):
        def hi(t, p, j):
            kind, n = FILLS[j]
            act.wait_ge(s_fill, NF * t + j + 1)
            if j == 0 and since(t, 2):
                act.wait_ge(s_v_out, 16 * (t - 1))
                act.wait_ge(s_scores, GROUPS * (t - 1))
            if kind == "v":
                src = ps_a[j % 2].rearrange("p (h d) -> p h d", d=HS)
                dst = v_tok[:, p, 8 * n:8 * n + 8, 0]
            elif kind == "q":
                if since(t, 1) or j >= 3:
                    act.wait_ge(s_fill_lo, NF * t + j - 1)
                src = ps_a[j % 2].rearrange("p (h t) -> p h t", h=4)
                dst = q_hi[:, j % 2]
            else:
                src = ps_a[j % 2].rearrange("p (h t) -> p h t", h=4)
                dst = k_hi[:, p, :, 4 * n:4 * n + 4].rearrange("p t h -> p h t")
            nc.scalar.activation(dst, src, ACT.Copy).then_inc(s_fill_hi, 1)

        def exps(t, g):
            n = GROUPS * t + g
            act.wait_ge(s_max, 2 * n + 2)
            nc.scalar.activation(nbias[:], nmax[:], ACT.Copy, scale=-SCORE_SCALE).then_inc(s_nbias, 1)
            act.wait_ge(s_nbias, n + 1)
            for q, (lo_, up_) in enumerate(((0, P), (P, 384))):
                nc.scalar.activation(probs[:, lo_:up_], ps_s[:, lo_:up_], ACT.Exp, bias=nbias[:, q:q + 1], scale=SCORE_SCALE,
                                     accum_out=den[:, g // 2 % 2, g % 2 * 2 + q:g % 2 * 2 + q + 1]).then_inc(s_exp, 1)

        def pt(t, g):
            act.wait_ge(s_pt, GROUPS * t + g + 1)
            nc.scalar.activation(pt_hi[:], ps_t[:, 0:384], ACT.Copy).then_inc(s_pt_hi, 1)

        def o_high(t, p, g):
            pair = 4 * t + g // 2
            act.wait_ge(s_o_norm, pair + 1)
            if g == 1 and since(t, 2):
                act.wait_ge(s_ot, 2 * (t - 1))
            nc.scalar.activation(o_st[:, p, 2 * (g - 1):2 * (g + 1), 0], o_norm[:], ACT.Copy).then_inc(s_o_hi, 1)

        def exp2(t, cc):
            act.wait_ge(s_shift, 2 * t + cc + 1)
            if since(t, 1) or cc:
                act.wait_ge(s_den2, 2 * t + cc)
            nc.scalar.activation(probs2[:], sm_shift[:], ACT.Exp, scale=SCORE2_SCALE).then_inc(s_exp2, 1)

        def stage_c(t, p, g):
            if g == 0:
                act.wait_ge(s_ot, 2 * t + 1)
                nc.scalar.activation(o_t[:, 0:64].rearrange("p t h -> p (t h)"), c5.bitcast(F16), ACT.Copy).then_inc(s_ot_a, 1)
            if g == 1:
                if p == 0:
                    act.wait_ge(s_kv2, half(t) + 1)
                    if since(t, 2):
                        act.wait_ge(s_bd, 4 * half(t))
                    nc.scalar.activation(k2[:, 0], c6[:, 0:KC * CTX].rearrange("p (c k) -> p c k", c=KC), ACT.Copy).then_inc(s_kv2_hi, 1)
                    nc.scalar.activation(v2[:, 0], c6[0:CTX, 256:512], ACT.Copy).then_inc(s_kv2_hi, 1)
            if g == 2:
                act.wait_ge(s_x1t, t + 1)
                nc.scalar.activation(x1_hi[:].rearrange("p c t -> p (c t)"), c6[:, 0:D], ACT.Copy, scale=X_UP).then_inc(s_x1_hi, 1)
            if g == 3:
                act.wait_ge(s_q2, t + 1)
                nc.scalar.activation(q2_hi[:].rearrange("p c t -> p (c t)"), c5[:, 0:D], ACT.Copy).then_inc(s_q2_hi, 1)
            if g in (5, 7):
                cc = (g - 5) // 2
                for j, bank in enumerate((c5, c6)):
                    act.wait_ge(s_t2, 4 * t + 2 * cc + j + 1)
                    nc.scalar.activation(pt2_hi[:, 4 * j:4 * j + 4].rearrange("p h t -> p (h t)"), bank[0:CTX, :], ACT.Copy).then_inc(s_t2_hi, 1)

        def stage_d(t, p, g):
            if g == 1:
                act.wait_ge(s_o2t, t + 1)
                nc.scalar.activation(o2_hi[:].rearrange("p c t -> p (c t)"), c7[:, 0:D], ACT.Copy).then_inc(s_o2_hi, 1)
            if g == 3:
                act.wait_ge(s_x2t, t + 1)
                nc.scalar.activation(x2_t[:].rearrange("p c t -> p (c t)"), c7[:, 0:D], ACT.Copy).then_inc(s_x2tc, 1)

        def step(s, p, stages):
            for g in range(GROUPS):
                if "B" in stages:
                    pt(s, g)
                if "C" in stages and g == 0:
                    o_high(s - 1, 1 - p, 7)
                fills = fills_of(s, p, g, stages)
                if g == 7 and fills:
                    hi(*fills.pop(0))
                if "C" in stages and g == 7:
                    exp2(s - 1, 1)
                if "B" in stages and g < GROUPS - 1:
                    exps(s, g + 1)
                elif "A" in stages and g == GROUPS - 1:
                    exps(s + 1, 0)
                if "B" in stages and g in (2, 4, 6):
                    o_high(s, p, g - 1)
                for t, q, j in fills[:EARLY[g]]:
                    hi(t, q, j)
                if "D" in stages and g < 3:
                    stage_d(s - 2, p, g)
                if "C" in stages:
                    stage_c(s - 1, 1 - p, g)
                for t, q, j in fills[EARLY[g]:]:
                    hi(t, q, j)
                if "D" in stages and g >= 3:
                    stage_d(s - 2, p, g)
                if "C" in stages and g == 4:
                    exp2(s - 1, 0)
                if "W" in stages and g == 1:
                    act.wait_ge(s_w_in, 16 * (s - 3))
                    act.wait_ge(s_w_out, 16 * (s - 3))
                    nc.scalar.activation(piece_pair[:, 0], piece[:], ACT.Copy, scale=WP_UP).then_inc(s_w_hi, 1)
                    act.wait_ge(s_w_hi, 2 * (s - 4) + 1)
                    nc.scalar.activation(piece[:], piece[:], ACT.Copy, scale=WP_UP).then_inc(s_w_hi, 1)

        steps(act, step)

    @block.vector
    def _(dve):
        stt = nc.vector.scalar_tensor_tensor

        def lo(t, p, j):
            kind, n = FILLS[j]
            dve.wait_ge(s_fill_hi, NF * t + j + 1)
            if kind == "v":
                src = ps_a[j % 2].rearrange("p (h d) -> p h d", d=HS)
                stt(out=v_tok[:, p, 8 * n:8 * n + 8, 1], in0=src, scalar=1.0, in1=v_tok[:, p, 8 * n:8 * n + 8, 0],
                    op0=ALU.mult, op1=ALU.subtract).then_inc(s_fill_lo, 1)
            elif kind == "q":
                src = ps_a[j % 2].rearrange("p (h t) -> p h t", h=4)
                stt(out=q_st[:, p, :, 4 * n:4 * n + 4].rearrange("p t h -> p h t"), in0=q_hi[:, j % 2], scalar=lo_rows[:, 0:1],
                    in1=src, op0=ALU.mult, op1=ALU.add).then_inc(s_fill_lo, 1)
            else:
                src = ps_a[j % 2].rearrange("p (h t) -> p h t", h=4)
                at = (slice(None), p, slice(None), slice(4 * n, 4 * n + 4))
                stt(out=k_lo[at].rearrange("p t h -> p h t"), in0=src, scalar=1.0, in1=k_hi[at].rearrange("p t h -> p h t"),
                    op0=ALU.mult, op1=ALU.subtract).then_inc(s_fill_lo, 1)

        def maxima(t, g):
            n = GROUPS * t + g
            dve.wait_ge(s_scores, n + 1)
            for q, (lo_, up_) in enumerate(((0, P), (P, 384))):
                nc.vector.tensor_reduce(nmax[:, q:q + 1], ps_s[:, lo_:up_], AX.X, ALU.max).then_inc(s_max, 1)

        def pt(t, g):
            dve.wait_ge(s_pt_hi, GROUPS * t + g + 1)
            nc.vector.tensor_tensor(pt_lo[:], ps_t[:, 0:384], pt_hi[:], ALU.subtract).then_inc(s_pt_lo, 1)

        def invert(t, g):
            dve.wait_ge(s_exp, 2 * (GROUPS * t + g) + 2)
            nc.vector.reciprocal(rden[:], den[:, g // 2 % 2]).then_inc(s_rden, 1)

        def normalise(t, g):
            pair = 4 * t + g // 2
            dve.wait_ge(s_rden, pair + 1)
            dve.wait_ge(s_pv, 2 * pair + 2)
            if since(t, 1) or g > 1:
                dve.wait_ge(s_o_lo, pair)
            nc.vector.tensor_tensor(o_norm[:], ps_o[:, 0:4 * HS].rearrange("p (q d) -> p q d", d=HS),
                                    rden[:].unsqueeze(2).to_broadcast([P, 4, HS]), ALU.mult).then_inc(s_o_norm, 1)

        def stats_of(t, ln, y, s_y, s_ln):
            dve.wait_ge(s_y, t + 1)
            nc.vector.bn_stats(stats[:, ln], y[:]).then_inc(s_ln, 1)

        def moments(t, ln, s_ln, s_mv):
            dve.wait_ge(s_ln, t + 1)
            dve.sem_inc(s_held_dve, 1)
            nc.vector.bn_aggr(mv[:, ln], stats[:, ln]).then_inc(s_mv, 1)

        def predicated(t, p, cc):
            dve.wait_ge(s_s2, 2 * t + cc + 1)
            dve.sem_inc(s_held_dve, 1)
            for j, bank in enumerate((c5, c6)):
                nc.vector.copy_predicated(sm[:, p, 4 * j:4 * j + 4], mask[:, p].unsqueeze(1).to_broadcast([P, 4, CTX]),
                                          bank[:, 0:4 * CTX].rearrange("p (h k) -> p h k", h=4)).then_inc(s_pred, 1)
            dve.wait_ge(s_pred, 4 * t + 2 * cc + 2)
            if since(t, 1) or cc:
                dve.wait_ge(s_shift, 2 * t + cc)
            nc.vector.tensor_reduce(mx2[:], sm[:, p], AX.X, ALU.max).then_inc(s_mx2, 1)

        def start(t, p, g):
            if g == 2:
                dve.wait_ge(s_rstd1, t + 1)
                nc.vector.tensor_scalar(x1[:, p], y1[:], mv[:, 0, 0:1], rstd[:, 0:1], ALU.subtract, ALU.mult).then_inc(s_x1, 1)

        def sums(t, p, cc):
            dve.wait_ge(s_exp2, 2 * t + cc + 1)
            nc.vector.tensor_reduce(den2[:, p, cc * HB:(cc + 1) * HB], probs2[:], AX.X, ALU.add).then_inc(s_den2, 1)

        def stage_c(t, p, g):
            if g == 0:
                dve.wait_ge(s_ot, 2 * t + 2)
                nc.vector.tensor_copy(o_t[:, 64:128].rearrange("p t h -> p (t h)"), c6.bitcast(F16)).then_inc(s_ot_d, 1)
            if g == 1:
                if p == 0:
                    dve.wait_ge(s_kv2_hi, 2 * (half(t) + 1))
                    nc.vector.tensor_tensor(k2[:, 1], c6[:, 0:KC * CTX].rearrange("p (c k) -> p c k", c=KC), k2[:, 0],
                                            ALU.subtract).then_inc(s_kv2_lo, 1)
                    nc.vector.tensor_tensor(v2[:, 1], c6[0:CTX, 256:512], v2[:, 0], ALU.subtract).then_inc(s_kv2_lo, 1)
                dve.wait_ge(s_proj, t + 1)
                dve.wait_ge(s_xb, t + 1)
                stt(out=y1[:], in0=c5[:, 0:D], scalar=1.0 / (QK_UP * WP_UP), in1=x_bias[:], op0=ALU.mult,
                    op1=ALU.add).then_inc(s_y1, 1)
            if g == 2:
                dve.wait_ge(s_x1_hi, t + 1)
                stt(out=x1_lo[:].rearrange("p c t -> p (c t)"), in0=c6[:, 0:D], scalar=X_UP,
                    in1=x1_hi[:].rearrange("p c t -> p (c t)"), op0=ALU.mult, op1=ALU.subtract).then_inc(s_x1_lo, 1)
            if g == 3:
                dve.wait_ge(s_q2_hi, t + 1)
                nc.vector.tensor_tensor(q2_lo[:].rearrange("p c t -> p (c t)"), c5[:, 0:D],
                                        q2_hi[:].rearrange("p c t -> p (c t)"), ALU.subtract).then_inc(s_q2_lo, 1)
            if g in (4, 6):
                predicated(t, p, (g - 4) // 2)
            if g == 6:
                sums(t, p, 0)
            if g in (5, 7):
                cc = (g - 5) // 2
                for j, bank in enumerate((c5, c6)):
                    dve.wait_ge(s_t2_hi, 4 * t + 2 * cc + j + 1)
                    at = pt2_hi[:, 4 * j:4 * j + 4].rearrange("p h t -> p (h t)")
                    nc.vector.tensor_tensor(pt2_lo[:, 4 * j:4 * j + 4].rearrange("p h t -> p (h t)"), bank[0:CTX, :], at,
                                            ALU.subtract).then_inc(s_t2_lo, 1)
                if cc == 1:
                    sums(t, p, 1)

        def stage_d(t, p, g):
            if g == 0:
                dve.wait_ge(s_rden2, t + 1)
                dve.wait_ge(s_pv2, 2 * t + 2)
                nc.vector.tensor_tensor(o2_norm[:], c7[:, 0:D].rearrange("p (h d) -> p h d", d=DK),
                                        rden2[:].unsqueeze(2).to_broadcast([P, H, DK]), ALU.mult).then_inc(s_o2n, 1)
            if g == 1:
                dve.wait_ge(s_o2_hi, t + 1)
                nc.vector.tensor_tensor(o2_lo[:].rearrange("p c t -> p (c t)"), c7[:, 0:D],
                                        o2_hi[:].rearrange("p c t -> p (c t)"), ALU.subtract).then_inc(s_o2_lo, 1)
            if g == 2:
                dve.wait_ge(s_proj2, t + 1)
                stt(out=y2[:], in0=c7[:, 0:D], scalar=1.0 / (QK_UP * WA_UP), in1=x1[:, p], op0=ALU.mult,
                    op1=ALU.add).then_inc(s_y2, 1)
            if g == 4:
                dve.wait_ge(s_lg, t + 1)
                nc.vector.tensor_copy(logits[:, bass.ds(t * E, E)], c7[:, 0:E]).then_inc(s_lgc, 1)

        def start_d(t, p, g):
            if g == 3:
                dve.wait_ge(s_rstd2, t + 1)
                if since(t, 2):
                    dve.wait_ge(s_out_x2[p], 16 * half(t))
                    dve.wait_ge(s_x2_lo, t - 1)
                nc.vector.tensor_scalar(x2[:, p], y2[:], mv[:, 1, 0:1], rstd[:, 1:2], ALU.subtract, ALU.mult).then_inc(s_x2, 1)

        def step(s, p, stages):
            for g in range(GROUPS):
                if "D" in stages and g == 0:
                    dve.wait_ge(s_den2, 2 * (s - 1))
                    nc.vector.reciprocal(rden2[:], den2[:, p]).then_inc(s_rden2, 1)
                if "C" in stages and g == 0:
                    normalise(s - 1, 7)
                fills = fills_of(s, p, g, stages)
                if g == 7 and fills:
                    lo(*fills.pop(0))
                if "B" in stages and g < GROUPS - 1:
                    maxima(s, g + 1)
                elif "A" in stages and g == GROUPS - 1:
                    maxima(s + 1, 0)
                if "B" in stages:
                    pt(s, g)
                if "B" in stages and g in (2, 4, 6):
                    normalise(s, g - 1)
                if "C" in stages:
                    start(s - 1, 1 - p, g)
                if "D" in stages:
                    start_d(s - 2, p, g)
                for t, q, j in fills[:EARLY[g]]:
                    lo(t, q, j)
                if "D" in stages and g < 3:
                    stage_d(s - 2, p, g)
                if "C" in stages:
                    stage_c(s - 1, 1 - p, g)
                if "D" in stages and g == 2:
                    stats_of(s - 2, 1, y2, s_y2, s_ln2)
                if "C" in stages and g == 1:
                    stats_of(s - 1, 0, y1, s_y1, s_ln1)
                for t, q, j in fills[EARLY[g]:]:
                    lo(t, q, j)
                if "D" in stages and g >= 3:
                    stage_d(s - 2, p, g)
                if "B" in stages and g % 2:
                    invert(s, g)
                if "D" in stages and g == 2:
                    moments(s - 2, 1, s_ln2, s_mv2)
                if "C" in stages and g == 1:
                    moments(s - 1, 0, s_ln1, s_mv1)

        nc.vector.memset(sm[:], NEG2).then_inc(s_neg, 1)
        dve.wait_ge(s_neg, 1)
        steps(dve, step)

    @block.gpsimd
    def _(pool):
        def split(pool, src, up, hi, lo, n, s_hi, s_lo):
            if since(n, 1):
                pool.wait_ge(s_lo, n)
            pool.sem_inc(s_held_pool, 1)
            nc.gpsimd.tensor_scalar(up, src, X_UP, None, ALU.mult).then_inc(s_hi, 1)
            pool.wait_ge(s_hi, 2 * n + 1)
            pool.sem_inc(s_held_pool, 1)
            nc.gpsimd.tensor_copy(hi, up).then_inc(s_hi, 1)
            pool.wait_ge(s_hi, 2 * n + 2)
            nc.gpsimd.tensor_tensor(lo, up, hi, ALU.subtract).then_inc(s_lo, 1)

        def split_x(t, p):
            pool.wait_ge(s_xt[p], 16 * (half(t) + 1))
            if since(t, 2):
                pool.wait_ge(s_fill, NF * (t - 1))
            split(pool, x_t[:, p], x_up[:], x_hi[:, p], x_lo[:, p], t, s_x_hi, s_x_lo)

        def split_o(t, p, g):
            pair = 4 * t + g // 2
            at = o_st[:, p, 2 * (g - 1):2 * (g + 1)]
            pool.wait_ge(s_o_hi, pair + 1)
            nc.gpsimd.tensor_tensor(at[:, :, 1], o_norm[:], at[:, :, 0], ALU.subtract).then_inc(s_o_lo, 1)

        def split_x2(t, p):
            pool.wait_ge(s_x2, t + 1)
            if since(t, 2):
                pool.wait_ge(s_out_pair[p], 16 * half(t))
            split(pool, x2[:, p], x2_up[:], x2_pair[:, p, 0], x2_pair[:, p, 1], t, s_x2_hi, s_x2_lo)

        def split_context(b):
            pool.wait_ge(s_ctx, 16 * (b + 1))
            if since(b, 1):
                pool.wait_ge(s_kv2, b)
            split(pool, ctx_t[:], ctx_up[:], c_hi[:], c_lo[:], b, s_c_hi, s_c_lo)

        def spread_k2(t, k):
            pool.wait_ge(s_kv2_lo, 2 * (half(t) + 1))
            for c in range(KC):
                nc.gpsimd.tensor_tensor(k2_bd[:, k, c], head_rows[:], k2[:, k, c].unsqueeze(1).to_broadcast([P, HB, CTX]),
                                        ALU.mult).then_inc(s_bd, 1)

        def bias_x(t, p):
            pool.wait_ge(s_xn[p], 16 * (half(t) + 1))
            if since(t, 1):
                pool.wait_ge(s_y1, t)
            nc.gpsimd.tensor_tensor(x_bias[:], x_nat[:, p], proj_b[:], ALU.add).then_inc(s_xb, 1)

        def inverse_deviation(t, ln, s_mv, s_var, s_rstd):
            pool.wait_ge(s_mv, t + 1)
            nc.gpsimd.tensor_tensor(var_eps[:, ln:ln + 1], mv[:, ln, 1:2], eps[:], ALU.add).then_inc(s_var, 1)
            pool.wait_ge(s_var, t + 1)
            nc.gpsimd.tensor_tensor(rstd[:, ln:ln + 1], var_eps[:, ln:ln + 1], neg_half[:], ALU.pow).then_inc(s_rstd, 1)

        def shift(t, p, cc):
            pool.wait_ge(s_mx2, 2 * t + cc + 1)
            if since(t, 1) or cc:
                pool.wait_ge(s_exp2, 2 * t + cc)
            nc.gpsimd.tensor_tensor(sm_shift[:], sm[:, p], mx2[:].unsqueeze(2).to_broadcast([P, HB, CTX]),
                                    ALU.subtract).then_inc(s_shift, 1)

        def step(s, p, stages):
            if isinstance(s, int) and s == -1:
                pool.sem_inc(s_w_out, 16)
                pool.sem_inc(s_w_lo, 1)
                split_x(0, 0)
                split_x(1, 1)
            for g in range(GROUPS):
                if "C" in stages and g == 0:
                    split_o(s - 1, 1 - p, 7)
                    bias_x(s - 1, 1 - p)
                if "B" in stages and g in (2, 4, 6):
                    split_o(s, p, g - 1)
                if "C" in stages and p == 1 and g in (1, 2):
                    spread_k2(s - 1, g - 1)
                if "C" in stages and g == 1:
                    inverse_deviation(s - 1, 0, s_mv1, s_var1, s_rstd1)
                if "D" in stages and g == 2:
                    inverse_deviation(s - 2, 1, s_mv2, s_var2, s_rstd2)
                if "D" in stages and g == 3:
                    split_x2(s - 2, p)
                if "C" in stages and g in (4, 6):
                    shift(s - 1, 1 - p, (g - 4) // 2)
                if "N" in stages and g == 4 and not (isinstance(s, int) and s < 0):
                    split_x(s + 2, p)
                if "B" in stages and g == 5 and p == 0:
                    split_context(half(s))
                if "W" in stages and g in (3, 5, 7):
                    n, c = s - 4, g // 2 - 1
                    at = slice(c * PIECE // 3, (c + 1) * PIECE // 3)
                    pool.wait_ge(s_w_hi, 2 * (n + 1))
                    nc.gpsimd.tensor_tensor(piece_pair[:, 1, at], piece[:, at], piece_pair[:, 0, at], ALU.subtract).then_inc(s_w_lo, 1)

        steps(pool, step)


def half(t):
    return t >> 1


SLOT_TILES = (2 * TOKENS + NE * (P - 1)) // P
QUAD = 4
CODES = 2 * TOKENS
H_UP = X_UP * WP_UP
G_UP = 16.0


def routing_block(nc, ctx, io, keep):
    def sb(name, shape, dt):
        return ctx.enter_context(nc.sbuf_tensor(name, shape, dt))

    def sem(name):
        return ctx.enter_context(nc.semaphore(name))

    T = TILES
    logits = keep["logits"]
    lg = logits[:].rearrange("p (t e) -> p t e", e=E)
    ps = ctx.enter_context(nc.psum_tensor("ps_r", [P, 4, 512], F32))
    tri = sb("tri", [P, P], F16)
    ones = sb("ones", [P, P], F16)
    iota_e = sb("iota_e", [P, E], F32)
    iota_lo = sb("iota_lo", [P, P], F32)
    iota_hi = sb("iota_hi", [P, SLOT_TILES], F32)
    iota_hi1 = sb("iota_hi1", [P, SLOT_TILES], F32)
    codes = sb("codes", [P, 2, T], F32)
    one_row = sb("one_row", [P, T], F32)
    mx = sb("r_mx", [P, T], F32)
    ex = sb("r_ex", [P, T, E], F32)
    sm = sb("r_sm", [P, T], F32)
    pr = sb("r_pr", [P, T, E], F32)
    m = sb("r_m", [P, 2, T], F32)
    tmp = sb("r_tmp", [P, T, E], F32)
    ix = sb("r_ix", [P, 2, T], F32)
    hot = sb("r_hot", [P, 2, T, E], F32)
    both = sb("r_both", [P, E, T], F32)
    elig = sb("r_elig", [P, NE, T], F32)
    elig16 = sb("r_elig16", [P, NE, T], F16)
    free = sb("r_free", [P, T], F32)
    cum = sb("r_cum", [P, NE, T], F32)
    pos = sb("r_pos", [P, NE, T], F32)
    kept = sb("r_kept", [P, NE, T], F32)
    over = sb("r_over", [P, E, T], F32)
    cnt = sb("r_cnt", [P, NE], F32)
    cnt_i = sb("r_cnt_i", [P, NE], I32)
    tiles = sb("r_tiles", [P, NE], F32)
    cumt = sb("r_cumt", [P, NE], F32)
    base = sb("r_base", [P, NE], F32)
    slot = sb("r_slot", [P, NE, T], F32)
    sk = sb("r_sk", [P, 2, T], F32)
    ovk = sb("r_ovk", [P, 2, T], F32)
    w = keep["weights"]
    tot = sb("r_tot", [P, T], F32)
    si = sb("r_si", [P, 2, T], I32)
    hi_i = sb("r_hi_i", [P, 2, T], I32)
    lo_i = sb("r_lo_i", [P, 2, T], I32)
    hi_f = sb("r_hi_f", [P, 2, T], F32)
    lo_f = sb("r_lo_f", [P, 2, T], F32)
    RING = 8
    ring_lo = sb("ring_lo", [P, RING, P], F32)
    ring_hi = sb("ring_hi", [P, RING, SLOT_TILES], F32)
    code = sb("r_code", [P, SLOT_TILES], F32)
    pad = sb("r_pad", [P, SLOT_TILES], F32)
    tokf = sb("r_tokf", [P, SLOT_TILES], F32)
    te = sb("r_te", [P, SLOT_TILES], F32)
    tok_i, dst_i, te_pack_i = keep["tok_i"], keep["dst_i"], keep["te_pack_i"]
    te_pack = sb("te_pack", [P, SLOT_TILES // QUAD], F32)

    s_const = sem("r_const")
    s_tri = sem("r_tri")
    s_ch = sem("r_chain")
    s_shift = sem("r_shifted")
    s_exp = sem("r_exped")
    s_elig = sem("r_elig_ready")
    s_pref = sem("r_prefixes")
    s_pref_used = sem("r_prefixes_used")
    s_hot = sem("r_hot_ready")
    s_place = sem("r_placed")
    s_w = keep["s_w"]
    block = ctx.enter_context(nc.Block())

    @block.sync
    def _(sp):
        for e in range(NE):
            for k in range(2):
                sp.dma_start(keep["wres"][:, k, e * WSIZE:(e + 1) * WSIZE], io["w_scr"][k, :, e * WSIZE:(e + 1) * WSIZE]).then_inc(s_w[e], 16)
        sp.dma_start(keep["b1"][:], io["b1T"]).then_inc(keep["s_b"], 16)
        sp.dma_start(keep["b2"][:], io["b2"].rearrange("(a n) -> a n", a=1).partition_broadcast(P)[:, 0, :]).then_inc(keep["s_b"], 16)

    @block.gpsimd
    def _(pool):
        g = nc.gpsimd
        g.memset(tri[:], 1.0).then_inc(s_tri, 1)
        g.memset(ones[:], 1.0).then_inc(s_const, 1)
        g.memset(one_row[:], 1.0).then_inc(s_const, 1)
        big = dict(allow_small_or_imprecise_dtypes=True)
        g.iota(iota_e[:], pattern=[[1, E]], base=0, channel_multiplier=0, **big).then_inc(s_const, 1)
        g.iota(iota_lo[:], pattern=[[1, P]], base=0, channel_multiplier=0, **big).then_inc(s_const, 1)
        g.iota(iota_hi[:], pattern=[[1, SLOT_TILES]], base=0, channel_multiplier=0, **big).then_inc(s_const, 1)
        g.iota(iota_hi1[:], pattern=[[1, SLOT_TILES]], base=1, channel_multiplier=0, **big).then_inc(s_const, 1)
        g.iota(codes[:], pattern=[[1, 2], [2 * P, T]], base=1, channel_multiplier=2, **big).then_inc(s_const, 1)
        pool.wait_ge(s_tri, 1)
        g.affine_select(out=tri[:], in_=tri[:], compare_op=ALU.is_ge, fill=0.0, base=0, pattern=[[1, P]],
                        channel_multiplier=-1).then_inc(s_const, 1)

    @block.scalar
    def _(act):
        act.wait_ge(s_shift, 1)
        nc.scalar.activation(ex[:].rearrange("p t e -> p (t e)"), pr[:].rearrange("p t e -> p (t e)"), ACT.Exp).then_inc(s_exp, 1)

    @block.tensor
    def _(pe):
        pe.wait_ge(s_const, 8)
        for e in range(NE):
            pe.wait_ge(s_elig, e + 1)
            if e:
                pe.wait_ge(s_pref_used, e)
            nc.tensor.matmul(ps[:, 0, 0:T], tri[:], elig16[:, e], start=True, stop=True)
            nc.tensor.matmul(ps[:, 0, T:2 * T], ones[:], elig16[:, e], start=True, stop=True).then_inc(s_pref, 1)
        for n in range(2 * T):
            pe.wait_ge(s_hot, 2 * n + 2)
            nc.tensor.matmul(ps[:, 1, 0:SLOT_TILES], ring_lo[:, n % RING], ring_hi[:, n % RING], start=(n == 0),
                             stop=(n == 2 * T - 1)).then_inc(s_place, 1)

    @block.vector
    def _(dve):
        v = nc.vector
        done = [0]

        def link(ins):
            done[0] += 1
            ins.then_inc(s_ch, 1)
            dve.wait_ge(s_ch, done[0])

        def wide(a, n=E):
            return a.unsqueeze(2).to_broadcast([P, T, n])

        link(v.tensor_reduce(mx[:], lg, AX.X, ALU.max))
        v.tensor_tensor(pr[:], lg, wide(mx[:]), ALU.subtract).then_inc(s_shift, 1)
        dve.wait_ge(s_exp, 1)
        link(v.tensor_reduce(sm[:], ex[:], AX.X, ALU.add))
        link(v.reciprocal(mx[:], sm[:]))
        link(v.tensor_tensor(pr[:], ex[:], wide(mx[:]), ALU.mult))
        dve.wait_ge(s_const, 8)
        ie = iota_e[:].unsqueeze(1).to_broadcast([P, T, E])
        for k in range(2):
            link(v.tensor_reduce(m[:, k], pr[:], AX.X, ALU.max))
            link(v.tensor_tensor(tmp[:], pr[:], wide(m[:, k]), ALU.is_lt))
            link(v.scalar_tensor_tensor(out=tmp[:], in0=tmp[:], scalar=100.0, in1=ie, op0=ALU.mult, op1=ALU.add))
            link(v.tensor_reduce(ix[:, k], tmp[:], AX.X, ALU.min))
            link(v.tensor_tensor(hot[:, k], ie, wide(ix[:, k]), ALU.is_equal))
            if k == 0:
                link(v.scalar_tensor_tensor(out=pr[:], in0=hot[:, 0], scalar=-4.0, in1=pr[:], op0=ALU.mult, op1=ALU.add))
        link(v.tensor_tensor(sm[:], m[:, 0], m[:, 1], ALU.add))
        link(v.tensor_scalar(sm[:], sm[:], 1e-9, None, ALU.max))
        link(v.reciprocal(mx[:], sm[:]))
        for k in range(2):
            link(v.tensor_tensor(w[:, k], m[:, k], mx[:], ALU.mult))
        link(v.tensor_tensor(both[:].rearrange("p e t -> p t e"), hot[:, 0], hot[:, 1], ALU.add))
        link(v.tensor_scalar(free[:], one_row[:], 1.0, None, ALU.mult))
        for e in range(NE):
            if e < E:
                link(v.tensor_tensor(elig[:, e], both[:, e], free[:], ALU.mult))
            else:
                link(v.tensor_scalar(elig[:, e], free[:], -1.0, 1.0, ALU.mult, ALU.add))
            v.tensor_copy(elig16[:, e], elig[:, e]).then_inc(s_elig, 1)
            dve.wait_ge(s_pref, e + 1)
            link(v.tensor_copy(tot[:], ps[:, 0, T:2 * T]))
            link(v.tensor_tensor_scan(cum[:, e], one_row[:], tot[:], 0.0, ALU.mult, ALU.add))
            link(v.tensor_tensor(pos[:, e], cum[:, e], tot[:], ALU.subtract))
            v.tensor_tensor(pos[:, e], pos[:, e], ps[:, 0, 0:T], ALU.add).then_inc(s_pref_used, 1)
            dve.wait_ge(s_pref_used, e + 1)
            if e < E:
                link(v.scalar_tensor_tensor(out=kept[:, e], in0=pos[:, e], scalar=float(CAP), in1=elig[:, e], op0=ALU.is_le, op1=ALU.mult))
                link(v.tensor_tensor(over[:, e], elig[:, e], kept[:, e], ALU.subtract))
                link(v.tensor_tensor(free[:], free[:], over[:, e], ALU.subtract))
                link(v.tensor_scalar(cnt[:, e:e + 1], cum[:, e, T - 1:T], float(CAP), None, ALU.min))
            else:
                link(v.tensor_scalar(cnt[:, e:e + 1], cum[:, e, T - 1:T], 1.0, None, ALU.mult))
        link(v.tensor_scalar(cnt[:], cnt[:], float(P - 1), None, ALU.add))
        link(v.tensor_copy(cnt_i[:], cnt[:]))
        link(v.tensor_single_scalar(cnt_i[:], cnt_i[:], 7, ALU.arith_shift_right))
        link(v.tensor_copy(tiles[:], cnt_i[:]))
        link(v.tensor_tensor_scan(cumt[:], one_row[:, 0:NE], tiles[:], 0.0, ALU.mult, ALU.add))
        link(v.tensor_tensor(base[:], cumt[:], tiles[:], ALU.subtract))
        link(v.tensor_scalar(base[:], base[:], float(P), None, ALU.mult))
        link(v.tensor_tensor(slot[:], pos[:], base[:].unsqueeze(2).to_broadcast([P, NE, T]), ALU.add))
        link(v.tensor_tensor(slot[:, 0:E], slot[:, 0:E], kept[:, 0:E], ALU.mult))
        for k in range(2):
            link(v.tensor_tensor(tmp[:], hot[:, k], slot[:, 0:E].rearrange("p e t -> p t e"), ALU.mult))
            link(v.tensor_reduce(sk[:, k], tmp[:], AX.X, ALU.add))
            link(v.tensor_tensor(tmp[:], hot[:, k], over[:].rearrange("p e t -> p t e"), ALU.mult))
            link(v.tensor_reduce(ovk[:, k], tmp[:], AX.X, ALU.add))
            link(v.tensor_tensor(tot[:], ovk[:, k], slot[:, E], ALU.mult))
            link(v.tensor_tensor(sk[:, k], sk[:, k], tot[:], ALU.add))
            link(v.tensor_tensor(w[:, k], w[:, k], free[:], ALU.mult))
            link(v.tensor_tensor(w[:, k], w[:, k], ovk[:, k], ALU.add))
        link(v.tensor_scalar(sk[:], sk[:], float(P - 1), None, ALU.add))
        link(v.tensor_copy(si[:], sk[:]))
        link(v.tensor_single_scalar(hi_i[:], si[:], 7, ALU.arith_shift_right))
        link(v.tensor_single_scalar(lo_i[:], si[:], P - 1, ALU.bitwise_and))
        link(v.tensor_copy(hi_f[:], hi_i[:]))
        link(v.tensor_copy(lo_f[:], lo_i[:]))
        for e in range(E):
            if e == 0:
                link(v.tensor_scalar(te[:], iota_hi[:], cumt[:, 0:1], None, ALU.is_ge))
            else:
                link(v.scalar_tensor_tensor(out=te[:], in0=iota_hi[:], scalar=cumt[:, e:e + 1], in1=te[:], op0=ALU.is_ge, op1=ALU.add))
        own = te[:].rearrange("p (b k) -> p k b", k=QUAD)
        link(v.scalar_tensor_tensor(out=te_pack[:], in0=own[:, 3], scalar=16.0, in1=own[:, 2], op0=ALU.mult, op1=ALU.add))
        for k in (1, 0):
            link(v.scalar_tensor_tensor(out=te_pack[:], in0=te_pack[:], scalar=16.0, in1=own[:, k], op0=ALU.mult, op1=ALU.add))
        link(v.tensor_scalar(te_pack[:], te_pack[:], 16.0, None, ALU.mult))
        link(v.tensor_tensor(te_pack[:, 1:], te_pack[:, 1:], own[:, 3, 0:SLOT_TILES // QUAD - 1], ALU.add))
        link(v.tensor_copy(te_pack_i[:], te_pack[:]))
        for n in range(2 * T):
            k, t = n // T, n % T
            if n >= RING:
                dve.wait_ge(s_place, n - RING + 1)
            v.tensor_scalar(ring_lo[:, n % RING], iota_lo[:], lo_f[:, k, t:t + 1], None, ALU.is_equal).then_inc(s_hot, 1)
            v.tensor_scalar(ring_hi[:, n % RING], iota_hi1[:], hi_f[:, k, t:t + 1], codes[:, k, t:t + 1], ALU.is_equal,
                            ALU.mult).then_inc(s_hot, 1)
        dve.wait_ge(s_place, 2 * T)
        link(v.tensor_copy(code[:], ps[:, 1, 0:SLOT_TILES]))
        link(v.tensor_scalar(pad[:], code[:], 0.0, float(CODES + 1), ALU.is_equal, ALU.mult))
        link(v.tensor_tensor(pad[:], pad[:], code[:], ALU.add))
        link(v.tensor_scalar(pad[:], pad[:], -1.0, None, ALU.add))
        link(v.tensor_copy(dst_i[:], pad[:]))
        link(v.tensor_scalar(tokf[:], code[:], -1.0, 0.0, ALU.add, ALU.max))
        link(v.tensor_copy(tok_i[:], tokf[:]))
        link(v.tensor_single_scalar(tok_i[:], tok_i[:], 1, ALU.arith_shift_right))


def experts_block(nc, ctx, io, keep):
    def sb(name, shape, dt):
        return ctx.enter_context(nc.sbuf_tensor(name, shape, dt))

    def sem(name):
        return ctx.enter_context(nc.semaphore(name))

    N = SLOT_TILES
    tok_i, dst_i, te_pack_i, wres, b1, b2 = (keep[n] for n in ("tok_i", "dst_i", "te_pack_i", "wres", "b1", "b2"))
    ident16 = keep["ident16"]
    s_w = keep["s_w"]
    s_held = keep["s_held"]
    rows_in = sb("rows_in", [P, 2, 1], I32)
    rows_out = sb("rows_out", [P, 2, 1], I32)
    xg = sb("xg", [P, 2, 2 * D], F16)
    xt = sb("xt", [P, 2, 2, KC, P], F16)
    act_g = sb("act_g", [P, 2, FC, P], F32)
    g_hi = sb("g_hi", [P, 2, FC, P], F16)
    g_lo = sb("g_lo", [P, 2, FC, P], F16)
    y = sb("e_y", [P, 2, D], F32)
    ps = ctx.enter_context(nc.psum_tensor("ps_e", [P, 8, 512], F32))
    ps_x = ps[:, 0, :].bitcast(F16)
    ps_y = [ps[:, 1, 0:D], ps[:, 2, 0:D]]
    (s_ri, s_ro, s_turn, s_xt, s_h, s_g, s_g_hi, s_g_lo, s_y, s_ye, s_sc0, s_sc1, s_ga0, s_ga1) = [
        sem("e_" + n) for n in "ri ro turn xt h g g_hi g_lo y ye sc0 sc1 ga0 ga1".split()]
    s_sc, s_ga = [s_sc0, s_sc1], [s_ga0, s_ga1]
    block = ctx.enter_context(nc.Block())

    def steps(eng, step, experts=None):
        def quad(b, *stages):
            e = experts(eng, b) if experts else [None] * 5
            for n in range(QUAD):
                step(QUAD * b + n, n % 2, stages[n], e[n:n + 2])
            return e

        step(-2, 0, "G", None)
        step(-1, 1, "GT", None)
        quad(0, "GTH", "GTHO", "GTHO", "GTHO")
        with eng.Fori(1, N // QUAD - 1, 1) as b:
            quad(b, "GTHO", "GTHO", "GTHO", "GTHO")
        last = quad(N // QUAD - 1, "GTHO", "THO", "THO", "HO")
        step(N, 0, "O", last[QUAD:])

    def since(t, n=0):
        return not (isinstance(t, int) and t < n)

    def experts(eng, b):
        packed = eng.value_load(te_pack_i[0:1, bass.ds(b, 1)], min_val=0, max_val=1 << 20)
        return [nc.s_assert_within(eng.snap((packed >> 4 * n) & 15), 0, NE - 1,
                                   skip_runtime_bounds_check_because="each expert is a sum of E comparisons")
                for n in range(QUAD + 1)]

    @block.gpsimd
    def _(pool):
        def gather(t, p):
            if since(t, 2):
                pool.wait_ge(s_ga[p], 16 * half(t))
            nc.gpsimd.tensor_copy(rows_in[:, p], tok_i[:, bass.ds(t, 1)]).then_inc(s_ri, 1)
            if since(t, 2):
                pool.wait_ge(s_turn, t - 1)
            pool.wait_ge(s_ri, t + 1)
            pool.sem_inc(s_held, 1)
            nc.gpsimd.indirect_dma_start(xg[:, p], None, io["pair_scr"],
                                         bass.IndirectOffsetOnAxis(ap=rows_in[:, p].bitcast(U32), axis=0)).then_inc(s_ga[p], 16)

        def step(k, p, stages, e):
            if "G" in stages:
                if isinstance(k, int) and k == -2:
                    gather(0, 0)
                gather(k + 3, 1 - p)
            if "O" in stages:
                t, q = k - 1, 1 - p
                if since(t, 2):
                    pool.wait_ge(s_sc[q], 16 * half(t))
                nc.gpsimd.tensor_copy(rows_out[:, q], dst_i[:, bass.ds(t, 1)]).then_inc(s_ro, 1)
                pool.wait_ge(s_ye, t + 1)
                pool.wait_ge(s_ro, t + 1)
                pool.sem_inc(s_held, 1)
                nc.gpsimd.indirect_dma_start(io["z_scr"], bass.IndirectOffsetOnAxis(ap=rows_out[:, q].bitcast(U32), axis=0), y[:, q], None,
                                             bounds_check=CODES - 1, oob_is_err=False).then_inc(s_sc[q], 16)

        steps(pool, step)
        for q in range(2):
            pool.wait_ge(s_sc[q], 16 * N // 2)

    @block.tensor
    def _(pe):
        mm = nc.tensor.matmul

        def turn(t, p):
            if since(t, 1):
                pe.wait_ge(s_xt, t)
            pe.wait_ge(s_ga[p], 16 * (half(t) + 1))
            for n in range(2 * KC):
                last = nc.tensor.transpose(ps_x[:, n * P:(n + 1) * P], xg[:, p, n * P:(n + 1) * P], ident16[:])
            last.then_inc(s_turn, 1)

        def hidden(t, p, e):
            pe.wait_ge(s_xt, t + 1)
            if since(t, 2):
                pe.wait_ge(s_g, FC * (t - 1))
            pe.sem_inc(keep["s_held_pe"], 1)
            w = wres[:, :, bass.ds(e * WSIZE, WSIZE)]
            for f in range(FC):
                out = ps[:, 3 + 2 * p + f // 4, (f % 4) * P:(f % 4 + 1) * P]
                todo = [(a, b, c) for c in range(KC) for a, b in ((0, 0), (1, 0), (0, 1))]
                for m, (a, b, c) in enumerate(todo):
                    last = mm(out, w[:, b, c * FF + f * P:c * FF + (f + 1) * P], xt[:, p, a, c], start=(m == 0), stop=(m == 5))
                last.then_inc(s_h, 1)

        def output(t, p, e):
            pe.wait_ge(s_g_lo, t + 1)
            if since(t, 2):
                pe.wait_ge(s_ye, t - 1)
            pe.sem_inc(keep["s_held_pe"], 1)
            w = wres[:, :, bass.ds(e * WSIZE, WSIZE)]
            for f in range(FC):
                for a, b in ((g_hi, 0), (g_hi, 1), (g_lo, 0)):
                    last = mm(ps_y[p], a[:, p, f], w[:, b, KC * FF + f * D:KC * FF + (f + 1) * D],
                              start=(f == 0 and a is g_hi and b == 0), stop=(f == FC - 1 and a is g_lo))
            last.then_inc(s_y, 1)

        def step(k, p, stages, e):
            if "T" in stages:
                turn(k + 1, 1 - p)
            if "H" in stages:
                hidden(k, p, e[1])
            if "O" in stages:
                output(k - 1, 1 - p, e[0])

        for e in range(NE):
            pe.wait_ge(s_w[e], 32)
        steps(pe, step, experts)

    @block.scalar
    def _(act):
        def step(k, p, stages, e):
            if "H" in stages:
                if since(k, 2):
                    act.wait_ge(s_g_lo, k - 1)
                bias = b1[:, bass.ds(e[1] * FC, FC)]
                for f in range(FC):
                    act.wait_ge(s_h, FC * k + (f // 4 + 1) * 4)
                    act.sem_inc(keep["s_held_act"], 1)
                    nc.scalar.activation(act_g[:, p, f], ps[:, 3 + 2 * p + f // 4, (f % 4) * P:(f % 4 + 1) * P], ACT.Gelu,
                                         bias=bias[:, f:f + 1], scale=1.0 / H_UP).then_inc(s_g, 1)

        act.wait_ge(keep["s_b"], 32)
        steps(act, step, experts)

    @block.vector
    def _(dve):
        def step(k, p, stages, e):
            if "T" in stages:
                t, q = k + 1, 1 - p
                dve.wait_ge(s_turn, t + 1)
                if since(t, 2):
                    dve.wait_ge(s_h, FC * (t - 1))
                nc.vector.tensor_copy(xt[:, q].rearrange("p k c n -> p (k c n)"), ps_x[:, 0:4 * P]).then_inc(s_xt, 1)
            if "O" in stages:
                t, q = k - 1, 1 - p
                dve.wait_ge(s_y, t + 1)
                if since(t, 2):
                    dve.wait_ge(s_sc[q], 16 * half(t))
                dve.sem_inc(keep["s_held_dve"], 1)
                nc.vector.scalar_tensor_tensor(out=y[:, q], in0=ps_y[q], scalar=1.0 / (G_UP * WP_UP), in1=b2[:, bass.ds(e[0] * D, D)],
                                               op0=ALU.mult, op1=ALU.add).then_inc(s_ye, 1)
            if "H" in stages:
                dve.wait_ge(s_g, FC * (k + 1))
                if since(k, 2):
                    dve.wait_ge(s_y, k - 1)
                nc.vector.tensor_scalar(g_hi[:, p], act_g[:, p], G_UP, None, ALU.mult).then_inc(s_g_hi, 1)
                dve.wait_ge(s_g_hi, k + 1)
                nc.vector.scalar_tensor_tensor(out=g_lo[:, p], in0=act_g[:, p], scalar=G_UP, in1=g_hi[:, p], op0=ALU.mult,
                                               op1=ALU.subtract).then_inc(s_g_lo, 1)

        dve.wait_ge(keep["s_b"], 32)
        steps(dve, step, experts)


def final_block(nc, ctx, io, keep):
    def sb(name, shape, dt):
        return ctx.enter_context(nc.sbuf_tensor(name, shape, dt))

    def sem(name):
        return ctx.enter_context(nc.semaphore(name))

    Q = 4
    N = TILES // Q
    w = keep["weights"]
    z = sb("f_z", [P, 2, Q, 2, D], F32)
    x2 = sb("f_x2", [P, 2, Q, D], F32)
    a = sb("f_a", [P, 2, Q, D], F32)
    s2 = sb("f_s2", [P, 2, Q, D], F32)
    out = sb("f_out", [P, 2, Q, D], F32)
    stats = sb("f_stats", [P, Q, 6], F32)
    mv = sb("f_mv", [P, 2, Q, 2], F32)
    ve = sb("f_ve", [P, 2, Q], F32)
    rstd = sb("f_rstd", [P, 2, Q], F32)
    nmr = sb("f_nmr", [P, 2, Q], F32)
    half4 = sb("f_half", [P, Q], F32)
    s_z = [sem("f_z0"), sem("f_z1")]
    s_out = [sem("f_o0"), sem("f_o1")]
    s_a, s_s, s_ch, s_ve, s_rstd, s_nmr, s_n, s_half = (sem("f_" + n) for n in "a s ch ve rstd nmr n half".split())
    block = ctx.enter_context(nc.Block())

    @block.sync
    def _(sp):
        for n in range(N):
            p = n % 2
            if n >= 2:
                sp.wait_ge(s_s, (n - 1) * Q)
            sp.dma_start(z[:, p], io["z_scr"].rearrange("(t p k) d -> p t k d", p=P, k=2)[:, n * Q:(n + 1) * Q]).then_inc(s_z[p], 16)
            sp.dma_start(x2[:, p], io["x2_scr"].rearrange("(t p) d -> p t d", p=P)[:, n * Q:(n + 1) * Q]).then_inc(s_z[p], 16)

    @block.scalar
    def _(act):
        def finish(n):
            p = n % 2
            act.wait_ge(s_nmr, n + 1)
            if n >= 2:
                act.wait_ge(s_out[p], 16 * (n // 2))
            for j in range(Q):
                nc.scalar.activation(out[:, p, j], s2[:, p, j], ACT.Identity, bias=nmr[:, p, j:j + 1], scale=rstd[:, p, j:j + 1]).then_inc(s_n, 1)
            act.wait_ge(s_n, (n + 1) * Q)
            act.dma_start(io["out"].rearrange("(t p) d -> p t d", p=P)[:, n * Q:(n + 1) * Q], out[:, p]).then_inc(s_out[p], 16)

        for n in range(N):
            p = n % 2
            act.wait_ge(s_z[p], 32 * (n // 2 + 1))
            if n >= 2:
                act.wait_ge(s_s, (n - 1) * Q)
            for j in range(Q):
                nc.scalar.activation(a[:, p, j], z[:, p, j, 0], ACT.Copy, scale=w[:, 0, n * Q + j:n * Q + j + 1]).then_inc(s_a, 1)
            if n >= 1:
                finish(n - 1)
        finish(N - 1)
        for p in range(2):
            act.wait_ge(s_out[p], 16 * (N // 2))

    @block.gpsimd
    def _(pool):
        nc.gpsimd.memset(half4[:], -0.5).then_inc(s_half, 1)
        pool.wait_ge(s_half, 1)
        for n in range(N):
            p = n % 2
            pool.wait_ge(s_ve, n + 1)
            nc.gpsimd.tensor_tensor(rstd[:, p], ve[:, p], half4[:], ALU.pow).then_inc(s_rstd, 1)

    @block.vector
    def _(dve):
        done = [0]

        def link(ins):
            done[0] += 1
            ins.then_inc(s_ch, 1)
            dve.wait_ge(s_ch, done[0])

        for n in range(N):
            p = n % 2
            if n >= 2:
                dve.wait_ge(s_n, (n - 1) * Q)
            for j in range(Q):
                dve.wait_ge(s_a, n * Q + j + 1)
                link(nc.vector.scalar_tensor_tensor(out=s2[:, p, j], in0=z[:, p, j, 1], scalar=w[:, 1, n * Q + j:n * Q + j + 1],
                                                    in1=a[:, p, j], op0=ALU.mult, op1=ALU.add))
                nc.vector.tensor_tensor(s2[:, p, j], s2[:, p, j], x2[:, p, j], ALU.add).then_inc(s_s, 1)
                dve.wait_ge(s_s, n * Q + j + 1)
                link(nc.vector.bn_stats(stats[:, j], s2[:, p, j]))
                link(nc.vector.bn_aggr(mv[:, p, j], stats[:, j]))
            nc.vector.tensor_scalar(ve[:, p], mv[:, p, :, 1], EPS, None, ALU.add).then_inc(s_ve, 1)
            dve.wait_ge(s_rstd, n + 1)
            nc.vector.scalar_tensor_tensor(out=nmr[:, p], in0=mv[:, p, :, 0], scalar=-1.0, in1=rstd[:, p], op0=ALU.mult,
                                           op1=ALU.mult).then_inc(s_nmr, 1)


def program(nc, io):
    with ExitStack() as ctx:
        def sb(name, shape, dt):
            return ctx.enter_context(nc.sbuf_tensor(name, shape, dt))

        keep = {
            "ident": sb("ident", [P, P], F32),
            "ident16": sb("ident16", [P, P], F16),
            "neg_half": sb("neg_half", [P, 1], F32),
            "logits": sb("logits", [P, TILES * E], F32),
            "weights": sb("weights", [P, 2, TILES], F32),
            "tok_i": sb("tok_i", [P, SLOT_TILES], I32),
            "dst_i": sb("dst_i", [P, SLOT_TILES], I32),
            "te_pack_i": sb("te_pack_i", [P, SLOT_TILES // QUAD], I32),
        }
        for n in ("s_held", "s_held_pe", "s_held_act", "s_held_dve", "s_held_pool", "s_held_sp", "s_b"):
            keep[n] = ctx.enter_context(nc.semaphore(n))
        keep["s_w"] = [ctx.enter_context(nc.semaphore("s_w%d" % e)) for e in range(NE)]
        with ExitStack() as phase:
            attention_block(nc, phase, io, keep)
        with ExitStack() as phase:
            keep["wres"] = phase.enter_context(nc.sbuf_tensor("wres", [P, 2, NE * WSIZE], F16))
            keep["b1"] = phase.enter_context(nc.sbuf_tensor("b1", [P, NE * FC], F32))
            keep["b2"] = phase.enter_context(nc.sbuf_tensor("b2", [P, NE * D], F32))
            with ExitStack() as part:
                routing_block(nc, part, io, keep)
            with ExitStack() as part:
                experts_block(nc, part, io, keep)
        with ExitStack() as phase:
            final_block(nc, phase, io, keep)


def kernel(**inputs):
    import numpy as _np
    import concourse.bacc as _bacc
    from concourse import mybir as _mybir
    from concourse.bass_utils import run_bass_kernel_spmd as _run

    nc = _bacc.Bacc("TRN2", target_bir_lowering=False, num_devices=1)
    a = {k: _np.asarray(v) for k, v in inputs.items()}
    up = _np.concatenate([a["L0_ffn_W1"], a["L0_ffn_fw1"][None]])
    down = _np.concatenate([a["L0_ffn_W2"], a["L0_ffn_fw2"][None]])
    moe_w = _np.concatenate([up.reshape(NE, KC, P, FF).transpose(2, 0, 1, 3).reshape(P, NE, -1),
                             down.reshape(NE, FC, P, D).transpose(2, 0, 1, 3).reshape(P, NE, -1)], axis=2)
    lay = {
        "x": a["x"].reshape(TOKENS, D),
        "xT": a["x"].reshape(TOKENS, D).T,
        "ctxT": a["ctx_1024"].transpose(2, 0, 1).reshape(D, BATCH * CTX),
        "mask": a["mask_1x1xSxS2_ik0"].reshape(SEQ, CTX),
        "wq": a["L0_attn_Wq"].transpose(1, 0, 2).reshape(D, H * HS),
        "wk": a["L0_attn_Wk"].transpose(1, 0, 2).reshape(D, H * HS),
        "wv": a["L0_attn_Wv"].transpose(1, 0, 2).reshape(D, H * HS),
        "proj": a["L0_attn_proj_w"].T,
        "proj_b": a["L0_attn_proj_b"],
        "xwq": a["L0_xattn_w_q"].T, "xwk": a["L0_xattn_w_k"].T, "xwv": a["L0_xattn_w_v"].T, "xwo": a["L0_xattn_w_o"].T,
        "wr": a["L0_ffn_Wr"].T,
        "moe_w": moe_w.reshape(P, NE * WSIZE),
        "b1T": _np.concatenate([a["L0_ffn_b1"], a["L0_ffn_fb1"][None]]).reshape(NE, FC, P).transpose(2, 0, 1).reshape(P, NE * FC),
        "b2": _np.concatenate([a["L0_ffn_b2"], a["L0_ffn_fb2"][None]]).reshape(NE * D),
    }
    arrays, io = {}, {}
    for name, v in lay.items():
        v = _np.ascontiguousarray(v)
        arrays["in_" + name] = v
        io[name] = nc.dram_tensor("in_" + name, v.shape, _mybir.dt.from_np(v.dtype), kind="ExternalInput").ap()
    for name, shape, dt in (("v_scr", (2, P, 2 * H * HS), F16), ("pair_scr", (TOKENS, 2 * D), F16), ("x2_scr", (TOKENS, D), F32),
                            ("z_scr", (CODES, D), F32), ("w_scr", (2, P, NE * WSIZE), F16)):
        io[name] = nc.dram_tensor(name, shape, dt, kind="Internal").ap()
    io["out"] = nc.dram_tensor("out_0", (TOKENS, D), F32, kind="ExternalOutput").ap()
    program(nc, io)
    r = _run(nc, [arrays], core_ids=[0])
    return r.results[0]["out_0"].reshape(BATCH, SEQ, D)
```
